# Optimizing a Trainium2 kernel written in Bass

```python
import numpy as np
import jax
import jax.numpy as jnp

def _softmax(x, axis=-1):
    return jax.nn.softmax(x, axis=axis)
def _gelu(x):
    return jax.nn.gelu(x, approximate=True)
def _silu(x):
    return jax.nn.silu(x)
def _sigmoid(x):
    return jax.nn.sigmoid(x)
def _layernorm(x, axis=-1, eps=1e-5):
    m = jnp.mean(x, axis=axis, keepdims=True)
    v = jnp.var(x, axis=axis, keepdims=True)
    return (x - m) / jnp.sqrt(v + eps)
def _scatter_add(tgt, idx, src, axis=0):
    return tgt.at[idx].add(src)
def _segment_sum(src, seg, n):
    return jax.ops.segment_sum(src, seg, n)

kernel_name = 'mk_conv_preact_d2_conv_nchw128_cc8285'

def setup_inputs(seed: int = 0):
    np.random.seed(seed)
    _w = jnp.asarray
    def _rec_inputs():
        import jax
        import jax.numpy as jnp
        _gk = jax.random.key(seed)
        x = 0.000266 + 1 * jax.random.normal(jax.random.fold_in(_gk, 1), (8, 128, 128, 128), jnp.float32)
        return x
    x = _rec_inputs()
    def _L0_conv_setup():
        import jax, jax.numpy as jnp
        import numpy as np
        FILTER_SIZE = 6
        LRELU_UPSAMPLE = 2
        SAMPLING_RATE = 128
        CUTOFF = 64
        HALF_WIDTH = 32
        SLOPE = 0.01
        UP = LRELU_UPSAMPLE
        NUM_TAPS = FILTER_SIZE * UP
        _pad_total = -1 + (NUM_TAPS - 1) * 2
        PAD_LO = (_pad_total + UP) // 2
        PAD_HI = _pad_total - PAD_LO

        def design_lowpass_filter(numtaps, cutoff, width, fs):
            nyq = 0.5 * fs
            wn = width / nyq
            a = 2.285 * (numtaps - 1) * np.pi * wn + 7.95
            if a > 50:
                beta = 0.1102 * (a - 8.7)
            elif a > 21:
                beta = 0.5842 * (a - 21) ** 0.4 + 0.07886 * (a - 21)
            else:
                beta = 0.0
            alpha = 0.5 * (numtaps - 1)
            m = np.arange(numtaps) - alpha
            c = cutoff / nyq
            h = c * np.sinc(c * m) * np.kaiser(numtaps, beta)
            h = h / h.sum()
            return jnp.asarray(h, dtype=jnp.float32)

        def _filtered_lrelu(x, f):
            N, C, H, W = x.shape
            xr = x.reshape(N * C, 1, H, W)
            fk = f[::-1].astype(x.dtype)
            dn = ('NCHW', 'OIHW', 'NCHW')
            g = jnp.asarray(UP, x.dtype)
            kv = (fk * g).reshape(1, 1, -1, 1)
            y = jax.lax.conv_general_dilated(xr, kv, (1, 1), ((PAD_LO, PAD_HI + UP - 1), (0, 0)), lhs_dilation=(UP, UP), dimension_numbers=dn)
            kh = (fk * g).reshape(1, 1, 1, -1)
            y = jax.lax.conv_general_dilated(y, kh, (1, 1), ((0, 0), (PAD_LO, PAD_HI + UP - 1)), dimension_numbers=dn)
            y = jnp.where(y >= 0, y, y * jnp.asarray(SLOPE, y.dtype))
            y = jax.lax.conv_general_dilated(y, fk.reshape(1, 1, -1, 1), (UP, 1), ((0, 0), (0, 0)), dimension_numbers=dn)
            y = jax.lax.conv_general_dilated(y, fk.reshape(1, 1, 1, -1), (1, UP), ((0, 0), (0, 0)), dimension_numbers=dn)
            Ho, Wo = (y.shape[-2], y.shape[-1])
            return y.reshape(N, C, Ho, Wo)
        key = jax.random.key(seed)
        x = jax.random.normal(key, (8, 128, 128, 128), dtype=jnp.float32)
        f = design_lowpass_filter(NUM_TAPS, CUTOFF, HALF_WIDTH * 2, SAMPLING_RATE * UP)
        return {'x': x, 'f': f}
    _L0_conv_all = _L0_conv_setup()
    _L0_conv_in = {k: v for k, v in _L0_conv_all.items() if k in ('f', )}
    del _L0_conv_all

    def _L1_conv_setup():
        import jax, jax.numpy as jnp
        import numpy as np
        MODES1 = 64
        MODES2 = 64

        def _c(t):
            return jax.lax.complex(t[..., 0], t[..., 1])

        def _contract_tt(xf, a, b, c, d):
            ac = _c(a)[0]
            bc = _c(b)
            cc = _c(c)
            dc = _c(d)[..., 0]
            o1 = jnp.einsum('jxk,ky,bcxy->jbcxy', cc, dc, xf)
            return jnp.einsum('oi,icj,jbcxy->boxy', ac, bc, o1)
        key = jax.random.key(seed)
        ks = jax.random.split(key, 9)
        std = 0.02
        inp = {'x': jax.random.normal(ks[0], (4, 128, 256, 256), dtype=jnp.float32), 'a1': std * jax.random.normal(ks[1], (1, 128, 64, 2), dtype=jnp.float32), 'b1': std * jax.random.normal(ks[2], (64, 128, 32, 2), dtype=jnp.float32), 'c1': std * jax.random.normal(ks[3], (32, 64, 32, 2), dtype=jnp.float32), 'd1': std * jax.random.normal(ks[4], (32, 64, 1, 2), dtype=jnp.float32), 'a2': std * jax.random.normal(ks[5], (1, 128, 64, 2), dtype=jnp.float32), 'b2': std * jax.random.normal(ks[6], (64, 128, 32, 2), dtype=jnp.float32), 'c2': std * jax.random.normal(ks[7], (32, 64, 32, 2), dtype=jnp.float32), 'd2': std * jax.random.normal(ks[8], (32, 64, 1, 2), dtype=jnp.float32)}
        return inp
    _L1_conv_all = _L1_conv_setup()
    _L1_conv_in = {k: v for k, v in _L1_conv_all.items() if k in ('a1', 'b1', 'c1', 'd1', 'a2', 'b2', 'c2', 'd2', )}
    del _L1_conv_all

    return {
        "x": x,
        "L0_conv_f": _L0_conv_in["f"],
        "L1_conv_a1": _L1_conv_in["a1"],
        "L1_conv_b1": _L1_conv_in["b1"],
        "L1_conv_c1": _L1_conv_in["c1"],
        "L1_conv_d1": _L1_conv_in["d1"],
        "L1_conv_a2": _L1_conv_in["a2"],
        "L1_conv_b2": _L1_conv_in["b2"],
        "L1_conv_c2": _L1_conv_in["c2"],
        "L1_conv_d2": _L1_conv_in["d2"],
    }

def reference(x, L0_conv_f, L1_conv_a1, L1_conv_b1, L1_conv_c1, L1_conv_d1, L1_conv_a2, L1_conv_b2, L1_conv_c2, L1_conv_d2):
    import jax
    import jax.numpy as jnp
    def _L0_conv_ref(x, f):
        import jax, jax.numpy as jnp
        import numpy as np
        FILTER_SIZE = 6
        LRELU_UPSAMPLE = 2
        SAMPLING_RATE = 128
        CUTOFF = 64
        HALF_WIDTH = 32
        SLOPE = 0.01
        UP = LRELU_UPSAMPLE
        NUM_TAPS = FILTER_SIZE * UP
        _pad_total = -1 + (NUM_TAPS - 1) * 2
        PAD_LO = (_pad_total + UP) // 2
        PAD_HI = _pad_total - PAD_LO

        def design_lowpass_filter(numtaps, cutoff, width, fs):
            nyq = 0.5 * fs
            wn = width / nyq
            a = 2.285 * (numtaps - 1) * np.pi * wn + 7.95
            if a > 50:
                beta = 0.1102 * (a - 8.7)
            elif a > 21:
                beta = 0.5842 * (a - 21) ** 0.4 + 0.07886 * (a - 21)
            else:
                beta = 0.0
            alpha = 0.5 * (numtaps - 1)
            m = np.arange(numtaps) - alpha
            c = cutoff / nyq
            h = c * np.sinc(c * m) * np.kaiser(numtaps, beta)
            h = h / h.sum()
            return jnp.asarray(h, dtype=jnp.float32)

        def _filtered_lrelu(x, f):
            N, C, H, W = x.shape
            xr = x.reshape(N * C, 1, H, W)
            fk = f[::-1].astype(x.dtype)
            dn = ('NCHW', 'OIHW', 'NCHW')
            g = jnp.asarray(UP, x.dtype)
            kv = (fk * g).reshape(1, 1, -1, 1)
            y = jax.lax.conv_general_dilated(xr, kv, (1, 1), ((PAD_LO, PAD_HI + UP - 1), (0, 0)), lhs_dilation=(UP, UP), dimension_numbers=dn)
            kh = (fk * g).reshape(1, 1, 1, -1)
            y = jax.lax.conv_general_dilated(y, kh, (1, 1), ((0, 0), (PAD_LO, PAD_HI + UP - 1)), dimension_numbers=dn)
            y = jnp.where(y >= 0, y, y * jnp.asarray(SLOPE, y.dtype))
            y = jax.lax.conv_general_dilated(y, fk.reshape(1, 1, -1, 1), (UP, 1), ((0, 0), (0, 0)), dimension_numbers=dn)
            y = jax.lax.conv_general_dilated(y, fk.reshape(1, 1, 1, -1), (1, UP), ((0, 0), (0, 0)), dimension_numbers=dn)
            Ho, Wo = (y.shape[-2], y.shape[-1])
            return y.reshape(N, C, Ho, Wo)
        return _filtered_lrelu(x, f)

    def _L1_conv_ref(x, a1, b1, c1, d1, a2, b2, c2, d2):
        import jax, jax.numpy as jnp
        import numpy as np
        MODES1 = 64
        MODES2 = 64

        def _c(t):
            return jax.lax.complex(t[..., 0], t[..., 1])

        def _contract_tt(xf, a, b, c, d):
            ac = _c(a)[0]
            bc = _c(b)
            cc = _c(c)
            dc = _c(d)[..., 0]
            o1 = jnp.einsum('jxk,ky,bcxy->jbcxy', cc, dc, xf)
            return jnp.einsum('oi,icj,jbcxy->boxy', ac, bc, o1)
        B, Cin, H, W = x.shape
        Cout = a1.shape[1]
        x_ft = jnp.fft.rfft2(x)
        out1 = _contract_tt(x_ft[:, :, :MODES1, :MODES2], a1, b1, c1, d1)
        out2 = _contract_tt(x_ft[:, :, -MODES1:, :MODES2], a2, b2, c2, d2)
        out_ft = jnp.zeros((B, Cout, H, W // 2 + 1), dtype=x_ft.dtype)
        out_ft = out_ft.at[:, :, :MODES1, :MODES2].set(out1)
        out_ft = out_ft.at[:, :, -MODES1:, :MODES2].set(out2)
        return jnp.fft.irfft2(out_ft, s=(H, W))

    def _gn(v, G=32, eps=1e-5):
        B_, C_, H_, W_ = v.shape
        g = v.reshape(B_, G, C_ // G, H_, W_)
        m = jnp.mean(g, axis=(2, 3, 4), keepdims=True)
        s = jnp.var(g, axis=(2, 3, 4), keepdims=True)
        return ((g - m) / jnp.sqrt(s + eps)).reshape(v.shape)

    def _ln_c(v, eps=1e-6):
        m = jnp.mean(v, axis=1, keepdims=True)
        s = jnp.var(v, axis=1, keepdims=True)
        return (v - m) / jnp.sqrt(s + eps)

    def _ln_t(v, eps=1e-5):
        m = jnp.mean(v, axis=-1, keepdims=True)
        s = jnp.var(v, axis=-1, keepdims=True)
        return (v - m) / jnp.sqrt(s + eps)

    def _to_tokens(v):
        B_, C_, H_, W_ = v.shape
        return v.reshape(B_, C_, H_ * W_).transpose(0, 2, 1)
    def _from_tokens(t, like):
        B_, C_, H_, W_ = like.shape
        return t.transpose(0, 2, 1).reshape(B_, C_, H_, W_)

    x = x + _L0_conv_ref(_gn(x), L0_conv_f)
    x = x + _L1_conv_ref(_gn(x), L1_conv_a1, L1_conv_b1, L1_conv_c1, L1_conv_d1, L1_conv_a2, L1_conv_b2, L1_conv_c2, L1_conv_d2)
    return x


_drawn_inputs = setup_inputs


def setup_inputs(seed=0):
    import zlib

    import numpy as np

    out = dict(_drawn_inputs(seed))
    spreads = {}
    factors = {'L1_conv_a1': 8.0,
     'L1_conv_b1': 8.0,
     'L1_conv_c1': 8.0,
     'L1_conv_d1': 8.0,
     'L1_conv_a2': 8.0,
     'L1_conv_b2': 8.0,
     'L1_conv_c2': 8.0,
     'L1_conv_d2': 8.0}
    for name, (base, spread) in spreads.items():
        noise = np.random.default_rng([zlib.crc32(name.encode()), seed]).standard_normal(out[name].shape)
        drawn = base * np.exp(spread * noise) if base else spread * noise
        out[name] = jnp.asarray(drawn.astype(out[name].dtype))
    for name, factor in factors.items():
        out[name] = (out[name] * factor).astype(out[name].dtype)
    return out
```

```python
from contextlib import ExitStack

import concourse.bass as bass
from concourse import mybir

F32 = mybir.dt.float32
ALU = mybir.AluOpType
ACT = mybir.ActivationFunctionType

B, C, H, W = 8, 128, 128, 128
TAPS = 12
UPS = 2 * H + TAPS - 2
TAIL = UPS - 2 * 128
IMGS = 4
QUADS = C // IMGS
NQ = B * QUADS
LO = 64
HI0 = (128 - TAPS + 2) // 2
TL0 = (256 - TAPS + 2) // 2
TLN = H - TL0
TR = IMGS * TAIL
MODES = 64
RANK_I, RANK_J = 64, 32
SLOPE = 0.01
EPS = 1e-5
UNITS6 = 16
HALF = 4


def wait(eng, sem, n):
    if isinstance(n, int) and n <= 0:
        return
    eng.wait_ge(sem, n)


def carry(eng, carried):
    eng.sem_inc(carried, 1)


def phase1(nc, x, ut_d, dt_d, dtail_d, mask_d, dfth_d, dftw_d, ones_d, x1, spec):
    with ExitStack() as ctx:
        def sb(name, shape):
            return ctx.enter_context(nc.sbuf_tensor(name, shape, F32))

        def sem(name):
            return ctx.enter_context(nc.semaphore(name))

        ring = ctx.enter_context(nc.psum_tensor("ring1", [128, 4, 2, 512], F32))
        ut = sb("ut", [128, UPS])
        dt = sb("dt", [128, LO + H - HI0])
        dtail = sb("dtail", [TR, IMGS * TLN + TLN])
        mask = sb("mask", [TR, TAIL, IMGS])
        dfth = sb("dfth", [128, 128])
        dftw = sb("dftw", [128, 2, 128])
        ones = sb("ones", [128, 128])
        xb = sb("xb", [128, 2, HALF, IMGS, W])
        g = sb("g", [128, 2, IMGS, W])
        A = sb("A", [128, 2, UPS, IMGS])
        Y = sb("Y", [128, 2, 2, UPS, IMGS])
        Yt = sb("Yt", [TR, 2, UPS])
        Yc = sb("Yc", [TR, 2, TAIL, IMGS])
        L = sb("L", [128, 2, 2, UPS])
        Lt = sb("Lt", [TR, UPS])
        Z = sb("Z", [128, 2, 2, IMGS, H])
        Zt = sb("Zt", [TR, 2, H])
        G = sb("G", [128, C, 128])
        psb = sb("psb", [128, 2, 512])
        sp_out = sb("sp_out", [128, 2, 2, 4, 128])
        st = sb("st", [128, HALF, 6])
        mv = sb("mv", [128, HALF, 2])
        sq = sb("sq", [128, HALF])
        var = sb("var", [128, HALF])
        std = sb("std", [128, HALF])
        rstd = sb("rstd", [128, 2, HALF])
        nmr = sb("nmr", [128, 2, HALF])
        st2 = sb("st2", [128, 2, 6])
        mv2 = sb("mv2", [128, 2])
        mvx = sb("mvx", [128, 2, QUADS, IMGS])
        tot = sb("tot", [128, 2 * HALF])
        tt2 = sb("tt2", [128, 5])
        rs2 = sb("rs2", [128, 3])

        c_ld = sem("c_ld")
        c_up = sem("c_up")
        x_ld = sem("x_ld")
        x1_st = sem("x1_st")
        sp_st = [sem("sp_st0"), sem("sp_st1")]
        g_ok = sem("g_ok")
        p_s1, p_s2, p_s3, p_tl, p_s4, p_s5, p_s6 = [sem(n) for n in ("p_s1", "p_s2", "p_s3", "p_tl", "p_s4", "p_s5", "p_s6")]
        e_s1 = sem("e_s1")
        e_l = sem("e_l")
        e_lt = sem("e_lt")
        e_s2 = sem("e_s2")
        e_s3 = sem("e_s3")
        e_t2 = sem("e_t2")
        e_yc = sem("e_yc")
        e_t3 = sem("e_t3")
        e_x1 = sem("e_x1")
        e_s5 = sem("e_s5")
        e_p6 = sem("e_p6")
        e_s6 = sem("e_s6")
        p_st = sem("p_st")
        carried = [sem(f"carried_{n}") for n in ("pool", "dve", "sp")]
        p_st2 = sem("p_st2")
        k_bn, k_mv, k_sq, k_e2 = [sem(n) for n in ("k_bn", "k_mv", "k_sq", "k_e2")]
        k_m2, k_var, k_rs, k_nm = [sem(n) for n in ("k_m2", "k_var", "k_rs", "k_nm")]
        b_bn, b_mv, b_x = [sem(n) for n in ("b_bn", "b_mv", "b_x")]
        b_m2, b_var, b_rs, b_dc = [sem(n) for n in ("b_m2", "b_var", "b_rs", "b_dc")]
        b_tot, b_dif, b_sd, k_sd = [sem(n) for n in ("b_tot", "b_dif", "b_sd", "k_sd")]

        x_v = x.rearrange("b c h w -> h (b c) w")
        x1_v = x1.rearrange("n h w -> h n w")
        ld_consts = ((ut, ut_d), (dt, dt_d), (dtail, dtail_d), (mask, mask_d), (dfth, dfth_d), (dftw, dftw_d),
                     (ones, ones_d))

        def pair_of(k, u):
            return (9 * k + u) % 4

        def x_par(k, back):
            return (k - back) // HALF % 2

        def steps(eng, first, body, last, drain):
            first()
            with eng.Fori(0, B - 1) as b:
                with eng.Fori(0, 3) as i:
                    body(4 * b + i, lambda k: 8 * i + 3 + k, None)
                body(4 * b + 3, lambda k: (27 + k) % QUADS, b)
            with eng.Fori(0, 3) as i:
                body(4 * (B - 1) + i, lambda k: 8 * i + 3 + k, None)
            last()
            drain()

        block = ctx.enter_context(nc.Block())

        @block.sync
        def _(sp):
            def load_half(h, par):
                for n in range(2):
                    sp.dma_start(xb[:, par, 2 * n:2 * n + 2].rearrange("p q i w -> p (q i) w"),
                                 x_v[:, bass.ds(16 * h + 8 * n, 8), :]).then_inc(x_ld, 16)

            def turn(h, par, more=True):
                sp.wait_ge(e_x1, 4 * h)
                sp.dma_start(x1_v[:, bass.ds(16 * (h - 1), 16), :],
                             xb[:, par].rearrange("p q i w -> p (q i) w")).then_inc(x1_st, 16)
                if more:
                    sp.wait_ge(p_s5, 4 * h)
                    sp.wait_ge(b_bn, 4 * h)
                    carry(sp, carried[2])
                    sp.wait_ge(x1_st, 16 * h)
                    load_half(h + 1, par)

            def store_spectra(b):
                with sp.Fori(0, UNITS6 // 2) as j2:
                    for e in range(2):
                        j = 2 * j2 + e
                        sp.wait_ge(e_s6, UNITS6 * b + j + 1)
                        for z in range(2):
                            sp.dma_start(spec[bass.ds(64 * z + 4 * j, 4), :, bass.ds(b, 1), :]
                                         .rearrange("s c o m -> c s (o m)"),
                                         sp_out[:, e, z]).then_inc(sp_st[e], 16)

            def first():
                for e in range(2):
                    sp.sem_inc(sp_st[e], 32)
                load_half(0, 0)
                for dst, src in ld_consts:
                    sp.dma_start(dst[:], src).then_inc(c_ld, 16)
                sp.wait_ge(x_ld, 32)
                load_half(1, 1)

            def body(t, jq, s6):
                turn(2 * t + 1, 0)
                turn(2 * t + 2, 1)
                if s6 is not None:
                    store_spectra(s6)

            def drain():
                turn(2 * 32, 1, more=False)
                store_spectra(B - 1)
                sp.wait_ge(x1_st, 16 * 64)
                for e in range(2):
                    sp.wait_ge(sp_st[e], 32 + 2 * 16 * B * UNITS6 // 2)

            steps(sp, first, body, lambda: turn(63, 0, more=False), drain)

        @block.gpsimd
        def _(pool):
            def half(h, par):
                for e in range(HALF):
                    q = 4 * h + e
                    if e == 0:
                        pool.wait_ge(k_nm, h + 1)
                    wait(pool, p_s1, 2 * (q - 1))
                    carry(pool, carried[0])
                    pool.tensor_scalar(g[:, e % 2].rearrange("p i w -> p (i w)"),
                                       xb[:, par, e].rearrange("p i w -> p (i w)"),
                                       rstd[:, par, e:e + 1], nmr[:, par, e:e + 1],
                                       ALU.mult, ALU.add).then_inc(g_ok, 1)

            def body(t, jq, s6):
                half(2 * t + 1, 1)
                half(2 * t + 2, 0)

            steps(pool, lambda: half(0, 0), body, lambda: half(63, 1), lambda: None)

        @block.tensor
        def _(pe):
            def step(q, k, up=True, down=True, rows=True, next_half=None, batch=None):
                e = k % 2
                if up:
                    pe.wait_ge(g_ok, q + 1)
                    for n in range(2):
                        wait(pe, e_s2, 4 * (q - 1) + 2 + n)
                        for m in range(2):
                            mm = pe.matmul(ring[:, pair_of(k, n), m, 0:UPS], g[:, e, 2 * n + m, :], ut[:],
                                           start=True, stop=True)
                        mm.then_inc(p_s1, 1)
                if down:
                    o = 1 - e
                    pe.wait_ge(e_s2, 4 * q)
                    pe.wait_ge(e_t2, q)
                    pe.wait_ge(e_yc, q)
                    for wt in range(2):
                        bank = ring[:, pair_of(k, 2), wt, :]
                        for m in range(IMGS):
                            pe.matmul(bank[:, 128 * m:128 * m + LO], Y[:, o, 0, 128 * wt:128 * wt + 128, m],
                                      dt[:, 0:LO], start=(m == 0), stop=False, skip_group_check=True)
                            pe.matmul(bank[:, 128 * m + HI0:128 * m + 128], Y[:, o, 1, 128 * wt:128 * wt + 128, m],
                                      dt[:, LO:], start=False, stop=False, skip_group_check=True)
                        mm = pe.matmul(bank.rearrange("p (i h) -> p i h", i=IMGS)[:, :, TL0:H],
                                       Yt[:, o, 128 * wt:128 * wt + 128], dtail[:, 0:IMGS * TLN],
                                       start=False, stop=True, skip_group_check=True)
                    mm.then_inc(p_s3, 1)
                tl = pair_of(k, 3)
                wait(pe, e_x1, q - 1)
                wait(pe, e_s5, q - 2)
                if next_half is not None:
                    pe.wait_ge(k_e2, next_half + 1)
                    pe.matmul(ring[:, tl, 1, 400:400 + 2 * HALF], ones[:], mv[:].rearrange("p q s -> p (q s)"),
                              start=True, stop=True).then_inc(p_st, 1)
                if batch is not None:
                    pe.wait_ge(b_x, QUADS * (batch + 1))
                    for s in range(2):
                        mm = pe.matmul(ring[:, tl, 1, 500 + s:501 + s], mvx[:, s].rearrange("p q i -> p (q i)"),
                                       ones[:, 0:1], start=True, stop=True)
                    mm.then_inc(p_st2, 1)
                if down:
                    zt = ring[0:TR, tl, 0, 0:H]
                    pe.matmul(zt[:, 0:LO], Y[:, o, 0, 256:UPS, :].rearrange("p t i -> p (t i)"), dt[:, 0:LO],
                              start=True, stop=False, skip_group_check=True)
                    pe.matmul(zt[:, HI0:H], Y[:, o, 1, 256:UPS, :].rearrange("p t i -> p (t i)"), dt[:, LO:],
                              start=False, stop=False, skip_group_check=True)
                    mm = pe.matmul(zt[:, TL0:H], Yc[:, o].rearrange("p t i -> p (t i)"), dtail[:, IMGS * TLN:],
                                   start=False, stop=True, skip_group_check=True)
                if up:
                    pe.wait_ge(e_s1, 2 * q + 2)
                    mm = pe.matmul(ring[0:TR, tl, 1, 0:UPS], A[:, e, 256:UPS, :].rearrange("p t i -> p (t i)"), ut[:], start=True, stop=True)
                if up or down:
                    mm.then_inc(p_tl, 1)
                if up:
                    for m in range(IMGS):
                        pr = pair_of(k, 4 + m)
                        if m == 2 and down:
                            pe.wait_ge(e_s3, q)
                        if m == 3:
                            pe.wait_ge(e_t2, q + 1)
                            wait(pe, e_t3, q)
                            if next_half is not None:
                                pe.wait_ge(k_nm, next_half + 1)
                            if batch is not None:
                                pe.wait_ge(b_tot, batch + 1)
                        for t in range(2):
                            mm = pe.matmul(ring[:, pr, t, 0:UPS], A[:, e, 128 * t:128 * t + 128, m], ut[:],
                                           start=True, stop=True)
                        mm.then_inc(p_s2, 1)
                pr = pair_of(k, 8)
                if up:
                    pe.wait_ge(e_s2, 4 * q + 1)
                if down:
                    pe.wait_ge(e_s3, q)
                    pe.wait_ge(e_t3, q)
                    bank = ring[:, pr, 0, :]
                    for m in range(IMGS):
                        pe.matmul(bank[:, 128 * m:128 * m + LO], Z[:, o, 0, m, :], dt[:, 0:LO],
                                  start=(m == 0), stop=False, skip_group_check=True)
                        pe.matmul(bank[:, 128 * m + HI0:128 * m + 128], Z[:, o, 1, m, :], dt[:, LO:],
                                  start=False, stop=False, skip_group_check=True)
                    pe.matmul(bank.rearrange("p (i w) -> p i w", i=IMGS)[:, :, TL0:W], Zt[:, o, :],
                              dtail[:, 0:IMGS * TLN], start=False, stop=True,
                              skip_group_check=True).then_inc(p_s4, 1)
                if rows:
                    pe.wait_ge(e_x1, q - 1)
                    for m in range(IMGS):
                        mm = pe.matmul(ring[:, pr, 1, 128 * m:128 * m + 128],
                                       xb[:, x_par(k, 2), (k - 2) % 4, m, :], dfth[:], start=True, stop=True)
                    mm.then_inc(p_s5, 1)

            def spectra(b):
                pe.wait_ge(e_s5, QUADS * (b + 1))
                for j in range(UNITS6):
                    pr = pair_of(5, 9 + j)
                    if j >= 4:
                        pe.wait_ge(e_s6, UNITS6 * b + j - 3)
                    for n in range(4):
                        s = 4 * j + n
                        pe.matmul(ring[:, pr, 0, 128 * n:128 * n + 128], G[:, :, s], dftw[:, 0, :],
                                  start=True, stop=True)
                        mm = pe.matmul(ring[:, pr, 1, 128 * n:128 * n + 128], G[:, :, 64 + s],
                                       dftw[:, 0 if s == 0 else 1, :], start=True, stop=True)
                    mm.then_inc(p_s6, 1)

            def drained(q, up):
                if up:
                    pe.wait_ge(e_s2, 4 * q + 4)
                pe.wait_ge(e_x1, min(q, NQ) if isinstance(q, int) else q)
                pe.wait_ge(e_s5, q - 1)

            def first():
                pe.wait_ge(c_ld, 16 * len(ld_consts))
                pe.wait_ge(c_up, 1)
                pe.wait_ge(k_e2, 1)
                pe.matmul(ring[:, 0, 1, 400:400 + 2 * HALF], ones[:], mv[:].rearrange("p q s -> p (q s)"),
                          start=True, stop=True).then_inc(p_st, 1)
                pe.wait_ge(k_nm, 1)
                for q in range(4):
                    step(q, q, down=q >= 1, rows=q >= 2, next_half=1 if q == 3 else None)

            def body(t, jq, s6):
                for k in range(8):
                    q = 8 * t + 4 + k
                    step(q, k + 4, next_half=2 * t + 2 if k == 3 else 2 * t + 3 if k == 7 else None,
                         batch=s6 if k == 5 else None)
                    if k == 5 and s6 is not None:
                        drained(q, True)
                        spectra(s6)
                        pe.wait_ge(e_s6, UNITS6 * (s6 + 1))

            def last():
                for k in range(4):
                    step(4 * 63 + k, k + 4)

            def drain():
                step(NQ, 0, up=False)
                step(NQ + 1, 1, up=False, down=False, batch=B - 1)
                drained(NQ + 1, False)
                spectra(B - 1)

            steps(pe, first, body, last, drain)

        @block.scalar
        def _(act):
            def root(h):
                act.wait_ge(k_var, h + 1)
                act.activation(std[:], var[:], ACT.Sqrt).then_inc(k_sd, 1)

            def step(q, k, up=True, rows=True, j5=None, next_half=None, batch=None):
                e = k % 2
                if up:
                    for n in range(2):
                        act.wait_ge(p_s1, 2 * q + n + 1)
                        act.activation(A[:, e, :, 2 * n:2 * n + 2].rearrange("p h i -> p i h"),
                                       ring[:, pair_of(k, n), :, 0:UPS], ACT.Copy).then_inc(e_s1, 1)
                    act.wait_ge(p_tl, q + 1)
                    act.activation(Lt[:], ring[0:TR, pair_of(k, 3), 1, 0:UPS], ACT.Copy,
                                   scale=SLOPE).then_inc(e_lt, 1)
                if next_half is not None:
                    root(next_half)
                if batch is not None:
                    act.wait_ge(b_var, batch + 1)
                    act.activation(tt2[:, 4:5], tt2[:, 3:4], ACT.Sqrt).then_inc(b_sd, 1)
                if up:
                    for m in range(IMGS):
                        act.wait_ge(p_s2, 4 * q + m + 1)
                        wait(act, e_s2, 4 * q + m - 1)
                        act.activation(L[:, m % 2], ring[:, pair_of(k, 4 + m), :, 0:UPS], ACT.Copy,
                                       scale=SLOPE).then_inc(e_l, 1)
                if rows:
                    act.wait_ge(p_s5, q - 1)
                    act.activation(G[:, bass.ds(4 * j5, IMGS), :],
                                   ring[:, pair_of(k, 8), 1, :].rearrange("p (i s) -> p i s", i=IMGS),
                                   ACT.Copy).then_inc(e_s5, 1)

            def spectra(b):
                act.wait_ge(b_dc, b + 1)
                for j in range(UNITS6):
                    act.wait_ge(p_s6, UNITS6 * b + j + 1)
                    if j >= 2:
                        act.wait_ge(e_s6, UNITS6 * b + j - 1)
                    act.activation(psb[:, j % 2, :], ring[:, pair_of(5, 9 + j), 0, :], ACT.Copy,
                                   scale=rs2[:, 0:1]).then_inc(e_p6, 1)

            def first():
                root(0)
                for q in range(4):
                    step(q, q, rows=q >= 2, j5=q - 2, next_half=1 if q == 3 else None)

            def body(t, jq, s6):
                for k in range(8):
                    j5 = jq(k) - 1 if s6 is None else (jq(k) - 1) % QUADS
                    step(8 * t + 4 + k, k + 4, j5=j5,
                         next_half=2 * t + 2 if k == 3 else 2 * t + 3 if k == 7 else None,
                         batch=s6 if k == 5 else None)
                    if k == 5 and s6 is not None:
                        spectra(s6)

            def last():
                for k in range(4):
                    step(252 + k, k + 4, j5=26 + k)

            def drain():
                step(NQ, 0, up=False, j5=30)
                step(NQ + 1, 1, up=False, j5=31, batch=B - 1)
                spectra(B - 1)

            steps(act, first, body, last, drain)

        @block.vector
        def _(dve):
            def stats_in(h, par):
                dve.wait_ge(x_ld, 32 * (h + 1))
                for n in range(HALF):
                    bn = dve.bn_stats(st[:, n, :], xb[:, par, n].rearrange("p i w -> p (i w)"))
                bn.then_inc(k_bn, 1)
                dve.wait_ge(k_bn, h + 1)
                wait(dve, p_st, h)
                carry(dve, carried[1])
                for n in range(HALF):
                    bn = dve.bn_aggr(mv[:, n, :], st[:, n, :])
                bn.then_inc(k_mv, 1)
                dve.wait_ge(k_mv, h + 1)
                dve.tensor_tensor(sq[:], mv[:, :, 0], mv[:, :, 0], ALU.mult).then_inc(k_sq, 1)
                dve.wait_ge(k_sq, h + 1)
                dve.tensor_tensor(mv[:, :, 1], mv[:, :, 1], sq[:], ALU.add).then_inc(k_e2, 1)

            def stats_out(h, par, pr):
                dve.wait_ge(p_st, h + 1)
                s = ring[:, pr, 1, 400:400 + 2 * HALF].rearrange("p (q s) -> p q s", s=2)
                dve.tensor_copy(tot[:], ring[:, pr, 1, 400:400 + 2 * HALF]).then_inc(k_m2, 1)
                s = tot[:].rearrange("p (q s) -> p q s", s=2)
                dve.wait_ge(k_m2, 3 * h + 1)
                dve.tensor_tensor(sq[:], s[:, :, 0], s[:, :, 0], ALU.mult).then_inc(k_m2, 1)
                dve.wait_ge(k_m2, 3 * h + 2)
                dve.tensor_tensor(var[:], s[:, :, 1], sq[:], ALU.subtract).then_inc(k_m2, 1)
                dve.wait_ge(k_m2, 3 * h + 3)
                dve.tensor_scalar(var[:], var[:], 0.0, EPS, ALU.max, ALU.add).then_inc(k_var, 1)
                dve.wait_ge(k_sd, h + 1)
                if not isinstance(h, int) or h >= 2:
                    dve.wait_ge(g_ok, 4 * (h - 1))
                dve.reciprocal(rstd[:, par, :], std[:]).then_inc(k_rs, 1)
                dve.wait_ge(k_rs, h + 1)
                dve.scalar_tensor_tensor(out=nmr[:, par, :], in0=s[:, :, 0], scalar=-1.0, in1=rstd[:, par, :],
                                         op0=ALU.mult, op1=ALU.mult).then_inc(k_nm, 1)

            def batch_out(b, pr):
                dve.wait_ge(p_st2, b + 1)
                dve.tensor_copy(tt2[:, 0:2], ring[:, pr, 1, 500:502]).then_inc(b_tot, 1)
                dve.wait_ge(b_tot, b + 1)
                dve.tensor_tensor(tt2[:, 2:3], tt2[:, 0:1], tt2[:, 0:1], ALU.mult).then_inc(b_m2, 1)
                dve.wait_ge(b_m2, b + 1)
                dve.tensor_tensor(tt2[:, 3:4], tt2[:, 1:2], tt2[:, 2:3], ALU.subtract).then_inc(b_dif, 1)
                dve.wait_ge(b_dif, b + 1)
                dve.tensor_scalar(tt2[:, 3:4], tt2[:, 3:4], 0.0, EPS, ALU.max, ALU.add).then_inc(b_var, 1)
                dve.wait_ge(b_sd, b + 1)
                dve.reciprocal(rs2[:, 0:1], tt2[:, 4:5]).then_inc(b_rs, 1)
                dve.wait_ge(b_rs, b + 1)
                dve.tensor_scalar(rs2[:, 1:2], rs2[:, 0:1], -1.0, None, ALU.mult)
                dve.scalar_tensor_tensor(out=rs2[:, 2:3], in0=tt2[:, 0:1], scalar=-float(H * W),
                                         in1=rs2[:, 0:1], op0=ALU.mult, op1=ALU.mult).then_inc(b_dc, 1)
                dve.wait_ge(b_dc, b + 1)

            def step(q, k, up=True, down=True, jq=None, next_in=None, next_out=None, batch_o=None):
                e, o = k % 2, 1 - k % 2
                if down:
                    dve.wait_ge(p_s3, q)
                    dve.tensor_copy(Z[:, o].rearrange("p t i h -> p t (i h)"),
                                    ring[:, pair_of(k, 2), :, :]).then_inc(e_s3, 1)
                    dve.wait_ge(p_tl, q + 1)
                    dve.tensor_copy(Zt[:, o, :], ring[0:TR, pair_of(k, 3), 0, 0:H]).then_inc(e_t3, 1)
                if up:
                    dve.wait_ge(e_lt, q + 1)
                    dve.tensor_tensor(Yt[:, e, :], ring[0:TR, pair_of(k, 3), 1, 0:UPS], Lt[:],
                                      ALU.max).then_inc(e_t2, 1)
                    dve.wait_ge(e_t2, q + 1)
                    dve.tensor_tensor(Yc[:, e], Yt[:, e, 256:UPS].unsqueeze(2).to_broadcast([TR, TAIL, IMGS]),
                                      mask[:], ALU.mult).then_inc(e_yc, 1)
                if next_out is not None:
                    stats_out(next_out[0], next_out[1], pair_of(k, 3))
                if batch_o is not None:
                    batch_out(batch_o, pair_of(k, 3))
                if up:
                    for m in range(IMGS):
                        dve.wait_ge(e_l, 4 * q + m + 1)
                        dve.tensor_tensor(Y[:, e, :, :, m], ring[:, pair_of(k, 4 + m), :, 0:UPS], L[:, m % 2],
                                          ALU.max).then_inc(e_s2, 1)
                if down:
                    xq = xb[:, x_par(k, 1), (k - 1) % 4].rearrange("p i w -> p (i w)")
                    dve.wait_ge(p_s4, q)
                    dve.wait_ge(g_ok, q)
                    dve.tensor_tensor(xq, xq, ring[:, pair_of(k, 8), 0, :], ALU.add).then_inc(e_x1, 1)
                    dve.wait_ge(e_x1, q)
                    dve.bn_stats(st2[:, e, :], xq).then_inc(b_bn, 1)
                    dve.wait_ge(b_bn, q)
                    carry(dve, carried[1])
                    dve.bn_aggr(mv2[:], st2[:, e, :]).then_inc(b_mv, 1)
                    dve.wait_ge(b_mv, q)
                    dve.tensor_copy(mvx[:, 0, bass.ds(jq, 1), :].rearrange("p o i -> p (o i)"),
                                    mv2[:, 0:1].to_broadcast([128, IMGS]))
                    dve.scalar_tensor_tensor(out=mvx[:, 1, bass.ds(jq, 1), :].rearrange("p o i -> p (o i)"),
                                             in0=mv2[:, 0:1].to_broadcast([128, IMGS]), scalar=mv2[:, 0:1],
                                             in1=mv2[:, 1:2].to_broadcast([128, IMGS]),
                                             op0=ALU.mult, op1=ALU.add).then_inc(b_x, 1)
                if next_in is not None:
                    stats_in(*next_in)

            def spectra(b):
                for j in range(UNITS6):
                    dve.wait_ge(sp_st[j % 2], 32 * (8 * b + j // 2 + 1))
                    dve.wait_ge(e_p6, UNITS6 * b + j + 1)
                    q_ps = ring[:, pair_of(5, 9 + j), 1, :].rearrange("p (n m) -> p n m", n=4)
                    p_sb = psb[:, j % 2, :].rearrange("p (n m) -> p n m", n=4)
                    n0 = 1 if j == 0 else 0
                    if j == 0:
                        dve.tensor_scalar(sp_out[:, 0, 1, 0, :], q_ps[:, 0, :], rs2[:, 0:1], None, ALU.mult)
                        dve.tensor_copy(sp_out[:, 0, 0, 0, 1:], p_sb[:, 0, 1:])
                        dve.tensor_tensor(sp_out[:, 0, 0, 0, 0:1], p_sb[:, 0, 0:1], rs2[:, 2:3], ALU.add)
                    dve.scalar_tensor_tensor(out=sp_out[:, j % 2, 0, n0:, :], in0=q_ps[:, n0:, :],
                                             scalar=rs2[:, 0:1], in1=p_sb[:, n0:, :], op0=ALU.mult, op1=ALU.add)
                    dve.scalar_tensor_tensor(out=sp_out[:, j % 2, 1, n0:, :], in0=q_ps[:, n0:, :],
                                             scalar=rs2[:, 1:2], in1=p_sb[:, n0:, :], op0=ALU.mult,
                                             op1=ALU.add).then_inc(e_s6, 1)

            def first():
                dve.wait_ge(c_ld, 16 * len(ld_consts))
                dve.tensor_scalar(ut[:], ut[:], 2.0, None, ALU.mult).then_inc(c_up, 1)
                stats_in(0, 0)
                stats_out(0, 0, 0)
                for q in range(4):
                    step(q, q, down=q >= 1, jq=q - 1, next_in=(1, 1) if q == 2 else None,
                         next_out=(1, 1) if q == 3 else None)

            def body(t, jq, s6):
                for k in range(8):
                    nh = (2 * t + 2, 0) if k < 4 else (2 * t + 3, 1)
                    step(8 * t + 4 + k, k + 4, jq=jq(k), next_in=nh if k % 4 == 2 else None,
                         next_out=nh if k % 4 == 3 else None,
                         batch_o=s6 if k == 5 else None)
                    if k == 5 and s6 is not None:
                        spectra(s6)

            def last():
                for k in range(4):
                    step(252 + k, k + 4, jq=27 + k)

            def drain():
                step(NQ, 0, up=False, jq=31)
                step(NQ + 1, 1, up=False, down=False, batch_o=B - 1)
                spectra(B - 1)

            steps(dve, first, body, last, drain)


def phase2(nc, spec, bst_d, cst_d, dst_d, am_d, fd):
    UN = 8
    with ExitStack() as ctx:
        def sb(name, shape):
            return ctx.enter_context(nc.sbuf_tensor(name, shape, F32))

        def sem(name):
            return ctx.enter_context(nc.semaphore(name))

        ring = ctx.enter_context(nc.psum_tensor("ring2", [128, 4, 2, 512], F32))
        bst = sb("bst", [128, RANK_I, 2, C])
        cst = sb("cst", [128, MODES, 2 * RANK_J])
        dst = sb("dst", [128, MODES])
        am = sb("am", [128, 2, 2, 2 * C])
        wall = sb("wall", [128, MODES, MODES])
        wcur = sb("wcur", [128, MODES])
        M = sb("M", [128, 2, MODES, 2 * RANK_I])
        xin = sb("xin", [128, 2, B, 2, MODES])
        pout = sb("pout", [128, 2, 2, B, MODES])
        ft = sb("ft", [128, 4, 2, 2, C])
        tmp = sb("tmp", [128, 2, 2, 2 * C])

        w_ld = sem("w_ld")
        w_neg = sem("w_neg")
        w_wp = sem("w_wp")
        w_we = sem("w_we")
        x_ld = [sem("xa_ld"), sem("xb_ld")]
        w_cur = [sem("wa_cur"), sem("wb_cur")]
        p_bld = sem("p_bld")
        e_ba = sem("e_ba")
        e_bv = sem("e_bv")
        p_app = [sem("p_app0"), sem("p_app1")]
        e_app = [sem("e_app0"), sem("e_app1")]
        p_out = sem("p_out")
        e_out = sem("e_out")
        f_st = [sem("f_st0"), sem("f_st1")]
        k_tmp = sem("k_tmp")

        lds = ((dst, dst_d), (cst, cst_d), (am, am_d), (bst, bst_d))
        block = ctx.enter_context(nc.Block())


        @block.sync
        def _(sp):
            def load(s, z):
                sp.dma_start(xin[:, z].rearrange("c b r y -> c (b r y)"),
                             spec[bass.ds(64 * z + s, 1)].rearrange("s c b m -> (s c) (b m)")).then_inc(x_ld[z], 16)

            def store(s, u):
                sp.wait_ge(e_out, 2 * s + u + 1)
                for n in range(2):
                    p = 2 * u + n
                    for z in range(2):
                        sp.dma_start(fd[128 * p:128 * p + 128, :, bass.ds(64 * z + s, 1), :]
                                     .rearrange("p r s o -> p r (s o)"), ft[:, p, z]).then_inc(f_st[u], 16)

            for z in range(2):
                load(0, z)
            for d, src in lds:
                sp.dma_start(d[:], src).then_inc(w_ld, 16)

            sp.wait_ge(p_app[0], 1)
            load(1, 0)
            with sp.Fori(1, MODES - 1) as s:
                sp.wait_ge(p_app[1], s)
                load(s, 1)
                store(s - 1, 0)
                store(s - 1, 1)
                sp.wait_ge(p_app[0], s + 1)
                load(s + 1, 0)
            sp.wait_ge(p_app[1], MODES - 1)
            load(MODES - 1, 1)
            for s in (MODES - 2, MODES - 1):
                store(s, 0)
                store(s, 1)
            for u in range(2):
                sp.wait_ge(f_st[u], 64 * MODES)

        @block.gpsimd
        def _(pool):
            pool.wait_ge(w_we, 8)

            def current(s, z):
                r = slice(64 * z, 64 * z + 64)
                pool.tensor_copy(wcur[r, :], wall[r, bass.ds(s, 1), :].rearrange("p s y -> p (s y)")).then_inc(w_cur[z], 1)

            current(0, 0)
            pool.wait_ge(w_cur[0], 1)
            current(0, 1)
            with pool.Fori(1, MODES) as s:
                pool.wait_ge(w_cur[1], s)
                pool.wait_ge(p_bld, 16 * s - 8)
                current(s, 0)
                pool.wait_ge(w_cur[0], s + 1)
                pool.wait_ge(p_bld, 16 * s)
                current(s, 1)

        @block.tensor
        def _(pe):
            pe.wait_ge(w_neg, 1)
            for u in range(8):
                if u >= 4:
                    pe.wait_ge(w_we, u - 3)
                for n in range(8):
                    for z in range(2):
                        r = slice(64 * z, 64 * z + 64)
                        mm = pe.matmul(ring[r, u % 4, 0, 64 * n:64 * n + 64], cst[r, 8 * u + n, :], dst[r, :],
                                       start=True, stop=True)
                mm.then_inc(w_wp, 1)
            pe.wait_ge(w_we, 8)

            def build(s, z):
                pe.wait_ge(w_cur[z], s + 1)
                r = slice(64 * z, 64 * z + 64)
                for u in range(8):
                    if u < 4:
                        if z == 0:
                            wait(pe, e_ba, 8 * s)
                            wait(pe, e_bv, 8 * s)
                            wait(pe, e_app[0], s)
                        else:
                            pe.wait_ge(e_bv, 8 * s + 4)
                            pe.wait_ge(e_ba, 8 * s + 4)
                            wait(pe, e_app[1], s)
                            if u >= 2:
                                wait(pe, e_out, 2 * s - 3 + u)
                    else:
                        if u % 2 == 0:
                            pe.wait_ge(e_ba, 8 * s + 4 * z + (u - 4) // 2 + 1)
                        else:
                            pe.wait_ge(e_bv, 8 * s + 4 * z + (u - 4) // 2 + 1)
                    pr = (11 * z + u) % 4
                    for n in range(16):
                        m = 16 * u + n
                        mm = pe.matmul(ring[:, pr, n // 8, 64 * (n % 8):64 * (n % 8) + 64],
                                       bst[r, m % 64, m // 64, :], wcur[r, :], start=True, stop=True)
                    mm.then_inc(p_bld, 1)

            def apply(s, z, n):
                pe.wait_ge(e_ba, 8 * s + 4 * z + 4)
                pe.wait_ge(e_bv, 8 * s + 4 * z + 4)
                if z == 0:
                    pe.wait_ge(e_ba, 8 * s + 7)
                elif not (isinstance(s, int) and s == MODES - 1):
                    pe.wait_ge(e_ba, 8 * s + 11)
                pe.wait_ge(x_ld[z], 16 * (s + 1))
                for y in range(MODES):
                    mm = pe.matmul(ring[:, n % 4, y // 32, 16 * (y % 32):16 * (y % 32) + 16], M[:, z, y, :],
                                   xin[:, z].rearrange("c b r y -> c (b r) y")[:, :, y], start=True, stop=True)
                mm.then_inc(p_app[z], 1)

            def out(s):
                for u in range(2):
                    if u == 0:
                        pe.wait_ge(e_app[0], s + 1)
                        pe.wait_ge(e_app[1], s + 1)
                    if not (isinstance(s, int) and s == MODES - 1):
                        pe.wait_ge(e_ba, 8 * s + 12)
                        pe.wait_ge(e_bv, 8 * s + 11)
                    for n in range(2):
                        p = 2 * u + n
                        for z in range(2):
                            for r in range(2):
                                mm = pe.matmul(ring[:, (9 + u) % 4, n, 256 * z:256 * z + 256],
                                               pout[:, z, r, 2 * p:2 * p + 2, :].rearrange("p b y -> p (b y)"),
                                               am[:, z, r, :], start=(r == 0), stop=(r == 1))
                    mm.then_inc(p_out, 1)

            build(0, 0)
            build(0, 1)
            apply(0, 0, 19)
            with pe.Fori(1, MODES) as s:
                build(s, 0)
                apply(s - 1, 1, 8)
                out(s - 1)
                build(s, 1)
                apply(s, 0, 19)
            apply(MODES - 1, 1, 8)
            out(MODES - 1)

        def evac_app(eng, copy, s, z, n):
            eng.wait_ge(p_app[z], s + 1)
            copy(pout[:, z].rearrange("p r b y -> p y b r"),
                 ring[:, n % 4].rearrange("p k (y b r) -> p (k y) b r", b=B, r=2)).then_inc(e_app[z], 1)

        def evac_build(eng, copy, s, z, par, done):
            for u in range(par, 8, 2):
                eng.wait_ge(p_bld, 16 * s + 8 * z + u + 1)
                copy(M[:, z, :, 16 * u:16 * u + 16].rearrange("c y m -> c m y"),
                     ring[:, (11 * z + u) % 4].rearrange("c k (m y) -> c (k m) y", y=MODES)).then_inc(done, 1)

        @block.scalar
        def _(act):
            def copy(dst_, src):
                return act.activation(dst_, src, ACT.Copy)

            def build(s, z):
                evac_build(act, copy, s, z, 0, e_ba)

            build(0, 0)
            build(0, 1)
            evac_app(act, copy, 0, 0, 19)
            with act.Fori(1, MODES) as s:
                build(s, 0)
                evac_app(act, copy, s - 1, 1, 8)
                build(s, 1)
                evac_app(act, copy, s, 0, 19)
            evac_app(act, copy, MODES - 1, 1, 8)

        @block.vector
        def _(dve):
            dve.wait_ge(w_ld, 16 * len(lds))
            for t in (32, 96):
                dve.tensor_scalar(cst[t:t + 32, :, 0:RANK_J], cst[t:t + 32, :, 0:RANK_J], -1.0, None, ALU.mult)
                dve.tensor_scalar(bst[t:t + 32, :, 0, :], bst[t:t + 32, :, 0, :], -1.0, None, ALU.mult)
            dve.tensor_scalar(am[64:, :, 0, 0:C], am[64:, :, 0, 0:C], -1.0, None, ALU.mult)
            dve.tensor_scalar(am[0:64, :, 1, 0:C], am[0:64, :, 1, 0:C], -1.0, None, ALU.mult)
            dve.tensor_scalar(am[64:, :, 1, :], am[64:, :, 1, :], -1.0, None, ALU.mult).then_inc(w_neg, 1)
            for u in range(8):
                dve.wait_ge(w_wp, u + 1)
                dve.tensor_copy(wall[:, 8 * u:8 * u + 8, :].rearrange("p s y -> p (s y)"),
                                ring[:, u % 4, 0, :]).then_inc(w_we, 1)

            def build(s, z):
                evac_build(dve, dve.tensor_copy, s, z, 1, e_bv)

            def out(s, alone=False):
                for u in range(2):
                    dve.wait_ge(p_out, 2 * s + u + 1)
                    if not alone:
                        dve.wait_ge(f_st[u], 64 * s)
                    ps = ring[:, (9 + u) % 4]
                    o = ft[:, 2 * u:2 * u + 2].rearrange("p n z r o -> p n z (r o)")
                    if alone:
                        dve.tensor_copy(o.rearrange("p n z m -> p n (z m)"), ps).then_inc(e_out, 1)
                    else:
                        a, b = ps[:, :, 0:256], ps[:, :, 256:512]
                        dve.tensor_copy(tmp[:, u], b).then_inc(k_tmp, 1)
                        dve.wait_ge(k_tmp, 2 * (s - 1) + u + 1)
                        dve.tensor_tensor(o[:, :, 0, :], a, tmp[:, u], ALU.add)
                        dve.tensor_tensor(o[:, :, 1, 0:C], tmp[:, u, :, C:], a[:, :, C:], ALU.subtract)
                        dve.tensor_tensor(o[:, :, 1, C:], a[:, :, 0:C], tmp[:, u, :, 0:C], ALU.subtract).then_inc(e_out, 1)

            build(0, 0)
            build(0, 1)
            build(1, 0)
            out(0, alone=True)
            build(1, 1)
            with dve.Fori(2, MODES) as s:
                build(s, 0)
                out(s - 1)
                build(s, 1)
            out(MODES - 1)


def phase3(nc, fd, x1, iy_d, ix_d, out):
    with ExitStack() as ctx:
        def sb(name, shape):
            return ctx.enter_context(nc.sbuf_tensor(name, shape, F32))

        def sem(name):
            return ctx.enter_context(nc.semaphore(name))

        ring = ctx.enter_context(nc.psum_tensor("ring3", [128, 8, 512], F32))
        iy = sb("iy", [128, W])
        ix = sb("ix", [128, H])
        F = sb("F", [128, 2, 128, C])
        zb = sb("zb", [128, 2, IMGS * W])
        xq = sb("xq", [128, 4, HALF * IMGS, W])

        c_ld = sem("c_ld3")
        f_ld = [sem("f_ld0"), sem("f_ld1")]
        r_ld = sem("r_ld")
        p_z = sem("p_z")
        e_z = sem("e_z")
        p_o = sem("p_o")
        e_o = sem("e_o")
        o_st = [sem("o_st0"), sem("o_st1")]

        fd_v = fd.rearrange("(b y) r s o -> b (y r) (s o)", b=B)
        x1_v = x1.rearrange("n h w -> h n w")
        out_v = out.rearrange("b c h w -> h (b c) w")
        block = ctx.enter_context(nc.Block())

        @block.sync
        def _(sp):
            sp.dma_start(iy[:], iy_d).then_inc(c_ld, 16)
            sp.dma_start(ix[:], ix_d).then_inc(c_ld, 16)

            def load_f(b, e):
                sp.dma_start(F[:, e].rearrange("p s o -> p (s o)"),
                             fd_v[bass.ds(b, 1)].rearrange("b p m -> (b p) m"),
                             max_dma_last_dim=16384).then_inc(f_ld[e], 16)

            def load_x(h, e):
                for n in range(2):
                    sp.dma_start(xq[:, e, 8 * n:8 * n + 8, :],
                                 x1_v[:, bass.ds(16 * h + 8 * n, 8), :]).then_inc(r_ld, 16)

            def store(h, e):
                sp.wait_ge(e_o, 4 * (h + 1))
                sp.dma_start(out_v[:, bass.ds(16 * h, 16), :], xq[:, e]).then_inc(o_st[e % 2], 16)

            for e in range(2):
                sp.sem_inc(o_st[e], 16)
            load_f(0, 0)
            load_x(0, 0)
            sp.wait_ge(r_ld, 32)
            load_x(1, 1)
            load_f(1, 1)
            with sp.Fori(0, B // 2 - 1) as b2:
                for b in range(2):
                    for n in range(8):
                        h = 16 * b2 + 8 * b + n
                        sp.wait_ge(r_ld, 32 * (h + 2))
                        sp.wait_ge(o_st[n % 2], 16 * (8 * b2 + 4 * b + n // 2 + 1))
                        load_x(h + 2, (n + 2) % 4)
                        store(h, n % 4)
                    sp.wait_ge(p_z, 32 * (2 * b2 + b + 1))
                    load_f(2 * b2 + b + 2, b)
            for h in range(48, 64):
                if h < 62:
                    sp.wait_ge(r_ld, 32 * (h + 2))
                    sp.wait_ge(o_st[h % 2], 16 * (h // 2 + 1))
                    load_x(h + 2, (h + 2) % 4)
                store(h, h % 4)
            for e in range(2):
                sp.wait_ge(o_st[e], 16 * 33)

        @block.tensor
        def _(pe):
            pe.wait_ge(c_ld, 32)

            def quad(q, k, first):
                if k < 64:
                    if k % 32 == 0:
                        pe.wait_ge(f_ld[k // 32], first)
                    wait(pe, e_z, q - 3)
                    for m in range(IMGS):
                        mm = pe.matmul(ring[:, k % 4, 128 * m:128 * m + 128], F[:, k // 32, :, 4 * (k % 32) + m],
                                       iy[:], start=True, stop=True)
                    mm.then_inc(p_z, 1)

            def final(q, k):
                pe.wait_ge(e_z, q + 1)
                wait(pe, e_o, q - 3)
                pe.matmul(ring[:, 4 + k % 4, :], ix[:], zb[:, k % 2, :], start=True, stop=True).then_inc(p_o, 1)

            def pair(b2, start):
                for k in range(64):
                    quad(64 * b2 + k, k, 16 * (b2 + 1))
                    if not (start and k == 0):
                        final(64 * b2 + k - 1, (k - 1) % 4)

            pair(0, True)
            with pe.Fori(1, B // 2) as b2:
                pair(b2, False)
            final(NQ - 1, 3)

        @block.scalar
        def _(act):
            def quad(q, k):
                act.wait_ge(p_z, q + 1)
                wait(act, p_o, q - 1)
                act.activation(zb[:, k % 2, :], ring[:, k % 4, :], ACT.Copy).then_inc(e_z, 1)

            for k in range(4):
                quad(k, k)
            with act.Fori(1, NQ // 4) as i:
                for k in range(4):
                    quad(4 * i + k, k)

        @block.vector
        def _(dve):
            with dve.Fori(0, NQ // 16) as i:
                for k in range(16):
                    h = 4 * i + k // 4
                    dve.wait_ge(r_ld, 32 * (h + 1))
                    dve.wait_ge(p_o, 16 * i + k + 1)
                    x_ = xq[:, k // 4, 4 * (k % 4):4 * (k % 4) + 4, :].rearrange("p i w -> p (i w)")
                    dve.tensor_tensor(x_, x_, ring[:, 4 + k % 4, :], ALU.add).then_inc(e_o, 1)


def program(nc, x, ut, dt, dtail, mask, dfth, dftw, ones, bst, cst, dst, am, iy, ix, out):
    x1 = nc.dram_tensor("x1", (B * C, H, W), F32, kind="Internal").ap()
    spec = nc.dram_tensor("spec", (128, C, B, 2 * MODES), F32, kind="Internal").ap()
    fd = nc.dram_tensor("fd", (B * MODES, 2, 128, C), F32, kind="Internal").ap()
    phase1(nc, x, ut, dt, dtail, mask, dfth, dftw, ones, x1, spec)
    phase2(nc, spec, bst, cst, dst, am, fd)
    phase3(nc, fd, x1, iy, ix, out)


def layouts(inputs):
    import numpy as np

    f = np.asarray(inputs["L0_conv_f"])
    ut = np.zeros((H, UPS), np.float32)
    dT = np.zeros((UPS, H), np.float32)
    for i in range(H):
        ut[i, 2 * i:2 * i + TAPS] = f
        dT[2 * i:2 * i + TAPS, i] = f[::-1]
    dt = np.concatenate([dT[0:128, 0:LO], dT[128:256, HI0:]], axis=1)
    tail = dT[256:, TL0:]
    dtail = np.zeros((TR, IMGS * TLN + TLN), np.float32)
    mask = np.zeros((TR, TAIL, IMGS), np.float32)
    for m in range(IMGS):
        dtail[m::IMGS, TLN * m:TLN * m + TLN] = tail
        dtail[m::IMGS, IMGS * TLN:] = tail
        mask[m::IMGS, :, m] = 1.0
    n = np.arange(128)
    ang = 2 * np.pi * (np.outer(n, n) % 128) / 128
    cos, sin = np.cos(ang), np.sin(ang)
    dfth = np.concatenate([cos[:, 0:65], sin[:, 1:64]], axis=1)
    cy, sy = cos[:, 0:MODES], sin[:, 0:MODES]
    dftw = np.stack([np.concatenate([cy, -sy], 1), np.concatenate([-sy, -cy], 1)], axis=1)
    wt = np.full((MODES, 1), 2.0 / (H * W))
    wt[0] = 1.0 / (H * W)
    iy = np.stack([wt * cy.T, -wt * sy.T], axis=1).reshape(128, W)
    f32 = lambda a: np.ascontiguousarray(a, dtype=np.float32)

    bst, cst, dst, am = [], [], [], []
    rows = (np.arange(64), np.concatenate([[0], np.arange(63, 0, -1)]))
    for z in range(2):
        a, b, c, d = (np.asarray(inputs[f"L1_conv_{n}{z + 1}"]) for n in "abcd")
        b = b.transpose(3, 2, 0, 1)
        bst += [np.stack([b[0], b[1]], axis=2), np.stack([b[1], b[0]], axis=2)]
        c = c[:, rows[z]].transpose(3, 2, 1, 0)
        cst += [np.concatenate([c[0], c[1]], axis=2), np.concatenate([c[1], c[0]], axis=2)]
        dst += [d[:, :, 0, 0], d[:, :, 0, 1]]
        a = a[0].transpose(2, 1, 0)
        ri, ir = np.concatenate([a[0], a[1]], axis=1), np.concatenate([a[1], a[0]], axis=1)
        am.append(np.stack([np.concatenate([ri, ir]), np.concatenate([ir, ri])], axis=1))
    return {
        "x": np.ascontiguousarray(inputs["x"]), "ut": ut, "dt": f32(dt), "dtail": dtail, "mask": mask,
        "dfth": f32(dfth), "dftw": f32(dftw), "ones": np.full((128, 128), 1.0 / 128, np.float32),
        "bst": np.ascontiguousarray(np.concatenate(bst)), "cst": np.ascontiguousarray(np.concatenate(cst)),
        "dst": np.ascontiguousarray(np.concatenate(dst)), "am": np.ascontiguousarray(np.stack(am, axis=1)),
        "iy": f32(iy), "ix": f32(dfth.T),
    }


def kernel(**inputs):
    import concourse.bacc as _bacc
    from concourse import mybir as _mybir
    from concourse.bass_utils import run_bass_kernel_spmd as _run

    nc = _bacc.Bacc("TRN2", target_bir_lowering=False, num_devices=1)
    arrays, args = {}, []
    for name, a in layouts(inputs).items():
        arrays[f"in_{name}"] = a
        args.append(nc.dram_tensor(f"in_{name}", a.shape, _mybir.dt.from_np(a.dtype), kind="ExternalInput").ap())
    args.append(nc.dram_tensor("out_0", (B, C, H, W), F32, kind="ExternalOutput").ap())
    program(nc, *args)
    return _run(nc, [arrays], core_ids=[0]).results[0]["out_0"]
```

```python
from contextlib import ExitStack

import concourse.bass as bass
from concourse import mybir

F32 = mybir.dt.float32
F16 = mybir.dt.float16
AX = mybir.AxisListType
ALU = mybir.AluOpType
ACT = mybir.ActivationFunctionType

B, C, H, W = 8, 128, 128, 128
TAPS = 12
UPS = 2 * H + TAPS - 2
TAIL = UPS - 2 * 128
IMGS = 4
QUADS = C // IMGS
NQ = B * QUADS
LO = 64
HI0 = (128 - TAPS + 2) // 2
TL0 = (256 - TAPS + 2) // 2
TLN = H - TL0
TR = IMGS * TAIL
MODES = 64
RANK_I, RANK_J = 64, 32
SLOPE = 0.01
EPS = 1e-5
X_SCALE = 128.0
UNITS6 = 16
HALF = 4


def wait(eng, sem, n):
    if isinstance(n, int) and n <= 0:
        return
    eng.wait_ge(sem, n)


def carry(eng, carried):
    eng.sem_inc(carried, 1)


def phase1(nc, x, ut_d, dt_d, dtail_d, mask_d, dfth_d, dftw_d, ones_d, x1, spec):
    with ExitStack() as ctx:
        def sb(name, shape):
            return ctx.enter_context(nc.sbuf_tensor(name, shape, F32))

        def sem(name):
            return ctx.enter_context(nc.semaphore(name))

        ring = ctx.enter_context(nc.psum_tensor("ring1", [128, 4, 2, 512], F32))
        ut = sb("ut", [128, UPS])
        dt = sb("dt", [128, LO + H - HI0])
        dtail = sb("dtail", [TR, IMGS * TLN + TLN])
        mask = sb("mask", [TR, TAIL, IMGS])
        dfth = sb("dfth", [128, 128])
        dftw = sb("dftw", [128, 2, 128])
        ones = sb("ones", [128, 128])
        xb = sb("xb", [128, 2, HALF, IMGS, W])
        g = sb("g", [128, 2, IMGS, W])
        A = sb("A", [128, 2, UPS, IMGS])
        Y = sb("Y", [128, 2, 2, UPS, IMGS])
        Yt = sb("Yt", [TR, 2, UPS])
        Yc = sb("Yc", [TR, 2, TAIL, IMGS])
        L = sb("L", [128, 2, 2, UPS])
        Lt = sb("Lt", [TR, UPS])
        Z = sb("Z", [128, 2, 2, IMGS, H])
        Zt = sb("Zt", [TR, 2, H])
        G = sb("G", [128, C, 128])
        psb = sb("psb", [128, 2, 512])
        sp_out = sb("sp_out", [128, 2, 2, 4, 128])
        st = sb("st", [128, HALF, 6])
        mv = sb("mv", [128, HALF, 2])
        sq = sb("sq", [128, HALF])
        var = sb("var", [128, HALF])
        std = sb("std", [128, HALF])
        rstd = sb("rstd", [128, 2, HALF])
        nmr = sb("nmr", [128, 2, HALF])
        st2 = sb("st2", [128, 2, 6])
        mv2 = sb("mv2", [128, 2])
        mvx = sb("mvx", [128, 2, QUADS, IMGS])
        tot = sb("tot", [128, 2 * HALF])
        tt2 = sb("tt2", [128, 5])
        rs2 = sb("rs2", [128, 3])

        c_ld = sem("c_ld")
        c_up = sem("c_up")
        x_ld = sem("x_ld")
        x1_st = sem("x1_st")
        sp_st = [sem("sp_st0"), sem("sp_st1")]
        g_ok = sem("g_ok")
        p_s1, p_s2, p_s3, p_tl, p_s4, p_s5, p_s6 = [sem(n) for n in ("p_s1", "p_s2", "p_s3", "p_tl", "p_s4", "p_s5", "p_s6")]
        e_s1 = sem("e_s1")
        e_l = sem("e_l")
        e_lt = sem("e_lt")
        e_s2 = sem("e_s2")
        e_s3 = sem("e_s3")
        e_t2 = sem("e_t2")
        e_yc = sem("e_yc")
        e_t3 = sem("e_t3")
        e_x1 = sem("e_x1")
        e_s5 = sem("e_s5")
        e_p6 = sem("e_p6")
        e_s6 = sem("e_s6")
        p_st = sem("p_st")
        carried = [sem(f"carried_{n}") for n in ("pool", "dve", "sp")]
        p_st2 = sem("p_st2")
        k_bn, k_mv, k_sq, k_e2 = [sem(n) for n in ("k_bn", "k_mv", "k_sq", "k_e2")]
        k_m2, k_var, k_rs, k_nm = [sem(n) for n in ("k_m2", "k_var", "k_rs", "k_nm")]
        b_bn, b_mv, b_x = [sem(n) for n in ("b_bn", "b_mv", "b_x")]
        b_m2, b_var, b_rs, b_dc = [sem(n) for n in ("b_m2", "b_var", "b_rs", "b_dc")]
        b_tot, b_dif, b_sd, k_sd = [sem(n) for n in ("b_tot", "b_dif", "b_sd", "k_sd")]

        x_v = x.rearrange("b c h w -> h (b c) w")
        x1_v = x1.rearrange("n h w -> h n w")
        ld_consts = ((ut, ut_d), (dt, dt_d), (dtail, dtail_d), (mask, mask_d), (dfth, dfth_d), (dftw, dftw_d),
                     (ones, ones_d))

        def pair_of(k, u):
            return (9 * k + u) % 4

        def x_par(k, back):
            return (k - back) // HALF % 2

        def steps(eng, first, body, last, drain):
            first()
            with eng.Fori(0, B - 1) as b:
                with eng.Fori(0, 3) as i:
                    body(4 * b + i, lambda k: 8 * i + 3 + k, None)
                body(4 * b + 3, lambda k: (27 + k) % QUADS, b)
            with eng.Fori(0, 3) as i:
                body(4 * (B - 1) + i, lambda k: 8 * i + 3 + k, None)
            last()
            drain()

        block = ctx.enter_context(nc.Block())

        @block.sync
        def _(sp):
            def load_half(h, par):
                for n in range(2):
                    sp.dma_start(xb[:, par, 2 * n:2 * n + 2].rearrange("p q i w -> p (q i) w"),
                                 x_v[:, bass.ds(16 * h + 8 * n, 8), :]).then_inc(x_ld, 16)

            def turn(h, par, more=True):
                sp.wait_ge(e_x1, 4 * h)
                sp.dma_start(x1_v[:, bass.ds(16 * (h - 1), 16), :],
                             xb[:, par].rearrange("p q i w -> p (q i) w")).then_inc(x1_st, 16)
                if more:
                    sp.wait_ge(p_s5, 4 * h)
                    sp.wait_ge(b_bn, 4 * h)
                    carry(sp, carried[2])
                    sp.wait_ge(x1_st, 16 * h)
                    load_half(h + 1, par)

            def store_spectra(b):
                with sp.Fori(0, UNITS6 // 2) as j2:
                    for e in range(2):
                        j = 2 * j2 + e
                        sp.wait_ge(e_s6, UNITS6 * b + j + 1)
                        for z in range(2):
                            sp.dma_start(spec[bass.ds(64 * z + 4 * j, 4), :, bass.ds(b, 1), :]
                                         .rearrange("s c o m -> c s (o m)"),
                                         sp_out[:, e, z]).then_inc(sp_st[e], 16)

            def first():
                for e in range(2):
                    sp.sem_inc(sp_st[e], 32)
                load_half(0, 0)
                for dst, src in ld_consts:
                    sp.dma_start(dst[:], src).then_inc(c_ld, 16)
                sp.wait_ge(x_ld, 32)
                load_half(1, 1)

            def body(t, jq, s6):
                turn(2 * t + 1, 0)
                turn(2 * t + 2, 1)
                if s6 is not None:
                    store_spectra(s6)

            def drain():
                turn(2 * 32, 1, more=False)
                store_spectra(B - 1)
                sp.wait_ge(x1_st, 16 * 64)
                for e in range(2):
                    sp.wait_ge(sp_st[e], 32 + 2 * 16 * B * UNITS6 // 2)

            steps(sp, first, body, lambda: turn(63, 0, more=False), drain)

        @block.gpsimd
        def _(pool):
            def half(h, par):
                for e in range(HALF):
                    q = 4 * h + e
                    if e == 0:
                        pool.wait_ge(k_nm, h + 1)
                    wait(pool, p_s1, 2 * (q - 1))
                    carry(pool, carried[0])
                    pool.tensor_scalar(g[:, e % 2].rearrange("p i w -> p (i w)"),
                                       xb[:, par, e].rearrange("p i w -> p (i w)"),
                                       rstd[:, par, e:e + 1], nmr[:, par, e:e + 1],
                                       ALU.mult, ALU.add).then_inc(g_ok, 1)

            def body(t, jq, s6):
                half(2 * t + 1, 1)
                half(2 * t + 2, 0)

            steps(pool, lambda: half(0, 0), body, lambda: half(63, 1), lambda: None)

        @block.tensor
        def _(pe):
            def step(q, k, up=True, down=True, rows=True, next_half=None, batch=None):
                e = k % 2
                if up:
                    pe.wait_ge(g_ok, q + 1)
                    for n in range(2):
                        wait(pe, e_s2, 4 * (q - 1) + 2 + n)
                        for m in range(2):
                            mm = pe.matmul(ring[:, pair_of(k, n), m, 0:UPS], g[:, e, 2 * n + m, :], ut[:],
                                           start=True, stop=True)
                        mm.then_inc(p_s1, 1)
                if down:
                    o = 1 - e
                    pe.wait_ge(e_s2, 4 * q)
                    pe.wait_ge(e_t2, q)
                    pe.wait_ge(e_yc, q)
                    for wt in range(2):
                        bank = ring[:, pair_of(k, 2), wt, :]
                        for m in range(IMGS):
                            pe.matmul(bank[:, 128 * m:128 * m + LO], Y[:, o, 0, 128 * wt:128 * wt + 128, m],
                                      dt[:, 0:LO], start=(m == 0), stop=False, skip_group_check=True)
                            pe.matmul(bank[:, 128 * m + HI0:128 * m + 128], Y[:, o, 1, 128 * wt:128 * wt + 128, m],
                                      dt[:, LO:], start=False, stop=False, skip_group_check=True)
                        mm = pe.matmul(bank.rearrange("p (i h) -> p i h", i=IMGS)[:, :, TL0:H],
                                       Yt[:, o, 128 * wt:128 * wt + 128], dtail[:, 0:IMGS * TLN],
                                       start=False, stop=True, skip_group_check=True)
                    mm.then_inc(p_s3, 1)
                tl = pair_of(k, 3)
                wait(pe, e_x1, q - 1)
                wait(pe, e_s5, q - 2)
                if next_half is not None:
                    pe.wait_ge(k_e2, next_half + 1)
                    pe.matmul(ring[:, tl, 1, 400:400 + 2 * HALF], ones[:], mv[:].rearrange("p q s -> p (q s)"),
                              start=True, stop=True).then_inc(p_st, 1)
                if batch is not None:
                    pe.wait_ge(b_x, QUADS * (batch + 1))
                    for s in range(2):
                        mm = pe.matmul(ring[:, tl, 1, 500 + s:501 + s], mvx[:, s].rearrange("p q i -> p (q i)"),
                                       ones[:, 0:1], start=True, stop=True)
                    mm.then_inc(p_st2, 1)
                if down:
                    zt = ring[0:TR, tl, 0, 0:H]
                    pe.matmul(zt[:, 0:LO], Y[:, o, 0, 256:UPS, :].rearrange("p t i -> p (t i)"), dt[:, 0:LO],
                              start=True, stop=False, skip_group_check=True)
                    pe.matmul(zt[:, HI0:H], Y[:, o, 1, 256:UPS, :].rearrange("p t i -> p (t i)"), dt[:, LO:],
                              start=False, stop=False, skip_group_check=True)
                    mm = pe.matmul(zt[:, TL0:H], Yc[:, o].rearrange("p t i -> p (t i)"), dtail[:, IMGS * TLN:],
                                   start=False, stop=True, skip_group_check=True)
                if up:
                    pe.wait_ge(e_s1, 2 * q + 2)
                    mm = pe.matmul(ring[0:TR, tl, 1, 0:UPS], A[:, e, 256:UPS, :].rearrange("p t i -> p (t i)"), ut[:], start=True, stop=True)
                if up or down:
                    mm.then_inc(p_tl, 1)
                if up:
                    for m in range(IMGS):
                        pr = pair_of(k, 4 + m)
                        if m == 2 and down:
                            pe.wait_ge(e_s3, q)
                        if m == 3:
                            pe.wait_ge(e_t2, q + 1)
                            wait(pe, e_t3, q)
                            if next_half is not None:
                                pe.wait_ge(k_nm, next_half + 1)
                            if batch is not None:
                                pe.wait_ge(b_tot, batch + 1)
                        for t in range(2):
                            mm = pe.matmul(ring[:, pr, t, 0:UPS], A[:, e, 128 * t:128 * t + 128, m], ut[:],
                                           start=True, stop=True)
                        mm.then_inc(p_s2, 1)
                pr = pair_of(k, 8)
                if up:
                    pe.wait_ge(e_s2, 4 * q + 1)
                if down:
                    pe.wait_ge(e_s3, q)
                    pe.wait_ge(e_t3, q)
                    bank = ring[:, pr, 0, :]
                    for m in range(IMGS):
                        pe.matmul(bank[:, 128 * m:128 * m + LO], Z[:, o, 0, m, :], dt[:, 0:LO],
                                  start=(m == 0), stop=False, skip_group_check=True)
                        pe.matmul(bank[:, 128 * m + HI0:128 * m + 128], Z[:, o, 1, m, :], dt[:, LO:],
                                  start=False, stop=False, skip_group_check=True)
                    pe.matmul(bank.rearrange("p (i w) -> p i w", i=IMGS)[:, :, TL0:W], Zt[:, o, :],
                              dtail[:, 0:IMGS * TLN], start=False, stop=True,
                              skip_group_check=True).then_inc(p_s4, 1)
                if rows:
                    pe.wait_ge(e_x1, q - 1)
                    for m in range(IMGS):
                        mm = pe.matmul(ring[:, pr, 1, 128 * m:128 * m + 128],
                                       xb[:, x_par(k, 2), (k - 2) % 4, m, :], dfth[:], start=True, stop=True)
                    mm.then_inc(p_s5, 1)

            def spectra(b):
                pe.wait_ge(e_s5, QUADS * (b + 1))
                for j in range(UNITS6):
                    pr = pair_of(5, 9 + j)
                    if j >= 4:
                        pe.wait_ge(e_s6, UNITS6 * b + j - 3)
                    for n in range(4):
                        s = 4 * j + n
                        pe.matmul(ring[:, pr, 0, 128 * n:128 * n + 128], G[:, :, s], dftw[:, 0, :],
                                  start=True, stop=True)
                        mm = pe.matmul(ring[:, pr, 1, 128 * n:128 * n + 128], G[:, :, 64 + s],
                                       dftw[:, 0 if s == 0 else 1, :], start=True, stop=True)
                    mm.then_inc(p_s6, 1)

            def drained(q, up):
                if up:
                    pe.wait_ge(e_s2, 4 * q + 4)
                pe.wait_ge(e_x1, min(q, NQ) if isinstance(q, int) else q)
                pe.wait_ge(e_s5, q - 1)

            def first():
                pe.wait_ge(c_ld, 16 * len(ld_consts))
                pe.wait_ge(c_up, 1)
                pe.wait_ge(k_e2, 1)
                pe.matmul(ring[:, 0, 1, 400:400 + 2 * HALF], ones[:], mv[:].rearrange("p q s -> p (q s)"),
                          start=True, stop=True).then_inc(p_st, 1)
                pe.wait_ge(k_nm, 1)
                for q in range(4):
                    step(q, q, down=q >= 1, rows=q >= 2, next_half=1 if q == 3 else None)

            def body(t, jq, s6):
                for k in range(8):
                    q = 8 * t + 4 + k
                    step(q, k + 4, next_half=2 * t + 2 if k == 3 else 2 * t + 3 if k == 7 else None,
                         batch=s6 if k == 5 else None)
                    if k == 5 and s6 is not None:
                        drained(q, True)
                        spectra(s6)
                        pe.wait_ge(e_s6, UNITS6 * (s6 + 1))

            def last():
                for k in range(4):
                    step(4 * 63 + k, k + 4)

            def drain():
                step(NQ, 0, up=False)
                step(NQ + 1, 1, up=False, down=False, batch=B - 1)
                drained(NQ + 1, False)
                spectra(B - 1)

            steps(pe, first, body, last, drain)

        @block.scalar
        def _(act):
            def root(h):
                act.wait_ge(k_var, h + 1)
                act.activation(std[:], var[:], ACT.Sqrt).then_inc(k_sd, 1)

            def step(q, k, up=True, rows=True, j5=None, next_half=None, batch=None):
                e = k % 2
                if up:
                    for n in range(2):
                        act.wait_ge(p_s1, 2 * q + n + 1)
                        act.activation(A[:, e, :, 2 * n:2 * n + 2].rearrange("p h i -> p i h"),
                                       ring[:, pair_of(k, n), :, 0:UPS], ACT.Copy).then_inc(e_s1, 1)
                    act.wait_ge(p_tl, q + 1)
                    act.activation(Lt[:], ring[0:TR, pair_of(k, 3), 1, 0:UPS], ACT.Copy,
                                   scale=SLOPE).then_inc(e_lt, 1)
                if next_half is not None:
                    root(next_half)
                if batch is not None:
                    act.wait_ge(b_var, batch + 1)
                    act.activation(tt2[:, 4:5], tt2[:, 3:4], ACT.Sqrt, scale=X_SCALE ** 2).then_inc(b_sd, 1)
                if up:
                    for m in range(IMGS):
                        act.wait_ge(p_s2, 4 * q + m + 1)
                        wait(act, e_s2, 4 * q + m - 1)
                        act.activation(L[:, m % 2], ring[:, pair_of(k, 4 + m), :, 0:UPS], ACT.Copy,
                                       scale=SLOPE).then_inc(e_l, 1)
                if rows:
                    act.wait_ge(p_s5, q - 1)
                    act.activation(G[:, bass.ds(4 * j5, IMGS), :],
                                   ring[:, pair_of(k, 8), 1, :].rearrange("p (i s) -> p i s", i=IMGS),
                                   ACT.Copy).then_inc(e_s5, 1)

            def spectra(b):
                act.wait_ge(b_dc, b + 1)
                for j in range(UNITS6):
                    act.wait_ge(p_s6, UNITS6 * b + j + 1)
                    if j >= 2:
                        act.wait_ge(e_s6, UNITS6 * b + j - 1)
                    act.activation(psb[:, j % 2, :], ring[:, pair_of(5, 9 + j), 0, :], ACT.Copy,
                                   scale=rs2[:, 0:1]).then_inc(e_p6, 1)

            def first():
                root(0)
                for q in range(4):
                    step(q, q, rows=q >= 2, j5=q - 2, next_half=1 if q == 3 else None)

            def body(t, jq, s6):
                for k in range(8):
                    j5 = jq(k) - 1 if s6 is None else (jq(k) - 1) % QUADS
                    step(8 * t + 4 + k, k + 4, j5=j5,
                         next_half=2 * t + 2 if k == 3 else 2 * t + 3 if k == 7 else None,
                         batch=s6 if k == 5 else None)
                    if k == 5 and s6 is not None:
                        spectra(s6)

            def last():
                for k in range(4):
                    step(252 + k, k + 4, j5=26 + k)

            def drain():
                step(NQ, 0, up=False, j5=30)
                step(NQ + 1, 1, up=False, j5=31, batch=B - 1)
                spectra(B - 1)

            steps(act, first, body, last, drain)

        @block.vector
        def _(dve):
            def stats_in(h, par):
                dve.wait_ge(x_ld, 32 * (h + 1))
                for n in range(HALF):
                    bn = dve.bn_stats(st[:, n, :], xb[:, par, n].rearrange("p i w -> p (i w)"))
                bn.then_inc(k_bn, 1)
                dve.wait_ge(k_bn, h + 1)
                wait(dve, p_st, h)
                carry(dve, carried[1])
                for n in range(HALF):
                    bn = dve.bn_aggr(mv[:, n, :], st[:, n, :])
                bn.then_inc(k_mv, 1)
                dve.wait_ge(k_mv, h + 1)
                dve.tensor_tensor(sq[:], mv[:, :, 0], mv[:, :, 0], ALU.mult).then_inc(k_sq, 1)
                dve.wait_ge(k_sq, h + 1)
                dve.tensor_tensor(mv[:, :, 1], mv[:, :, 1], sq[:], ALU.add).then_inc(k_e2, 1)

            def stats_out(h, par, pr):
                dve.wait_ge(p_st, h + 1)
                s = ring[:, pr, 1, 400:400 + 2 * HALF].rearrange("p (q s) -> p q s", s=2)
                dve.tensor_copy(tot[:], ring[:, pr, 1, 400:400 + 2 * HALF]).then_inc(k_m2, 1)
                s = tot[:].rearrange("p (q s) -> p q s", s=2)
                dve.wait_ge(k_m2, 3 * h + 1)
                dve.tensor_tensor(sq[:], s[:, :, 0], s[:, :, 0], ALU.mult).then_inc(k_m2, 1)
                dve.wait_ge(k_m2, 3 * h + 2)
                dve.tensor_tensor(var[:], s[:, :, 1], sq[:], ALU.subtract).then_inc(k_m2, 1)
                dve.wait_ge(k_m2, 3 * h + 3)
                dve.tensor_scalar(var[:], var[:], 0.0, EPS, ALU.max, ALU.add).then_inc(k_var, 1)
                dve.wait_ge(k_sd, h + 1)
                if not isinstance(h, int) or h >= 2:
                    dve.wait_ge(g_ok, 4 * (h - 1))
                dve.reciprocal(rstd[:, par, :], std[:]).then_inc(k_rs, 1)
                dve.wait_ge(k_rs, h + 1)
                dve.scalar_tensor_tensor(out=nmr[:, par, :], in0=s[:, :, 0], scalar=-1.0, in1=rstd[:, par, :],
                                         op0=ALU.mult, op1=ALU.mult).then_inc(k_nm, 1)

            def batch_out(b, pr):
                dve.wait_ge(p_st2, b + 1)
                dve.tensor_copy(tt2[:, 0:2], ring[:, pr, 1, 500:502]).then_inc(b_tot, 1)
                dve.wait_ge(b_tot, b + 1)
                dve.tensor_tensor(tt2[:, 2:3], tt2[:, 0:1], tt2[:, 0:1], ALU.mult).then_inc(b_m2, 1)
                dve.wait_ge(b_m2, b + 1)
                dve.tensor_tensor(tt2[:, 3:4], tt2[:, 1:2], tt2[:, 2:3], ALU.subtract).then_inc(b_dif, 1)
                dve.wait_ge(b_dif, b + 1)
                dve.tensor_scalar(tt2[:, 3:4], tt2[:, 3:4], 0.0, EPS, ALU.max, ALU.add).then_inc(b_var, 1)
                dve.wait_ge(b_sd, b + 1)
                dve.reciprocal(rs2[:, 0:1], tt2[:, 4:5]).then_inc(b_rs, 1)
                dve.wait_ge(b_rs, b + 1)
                dve.tensor_scalar(rs2[:, 1:2], rs2[:, 0:1], -1.0, None, ALU.mult)
                dve.scalar_tensor_tensor(out=rs2[:, 2:3], in0=tt2[:, 0:1], scalar=-float(H * W),
                                         in1=rs2[:, 0:1], op0=ALU.mult, op1=ALU.mult).then_inc(b_dc, 1)
                dve.wait_ge(b_dc, b + 1)

            def step(q, k, up=True, down=True, jq=None, next_in=None, next_out=None, batch_o=None):
                e, o = k % 2, 1 - k % 2
                if down:
                    dve.wait_ge(p_s3, q)
                    dve.tensor_copy(Z[:, o].rearrange("p t i h -> p t (i h)"),
                                    ring[:, pair_of(k, 2), :, :]).then_inc(e_s3, 1)
                    dve.wait_ge(p_tl, q + 1)
                    dve.tensor_copy(Zt[:, o, :], ring[0:TR, pair_of(k, 3), 0, 0:H]).then_inc(e_t3, 1)
                if up:
                    dve.wait_ge(e_lt, q + 1)
                    dve.tensor_tensor(Yt[:, e, :], ring[0:TR, pair_of(k, 3), 1, 0:UPS], Lt[:],
                                      ALU.max).then_inc(e_t2, 1)
                    dve.wait_ge(e_t2, q + 1)
                    dve.tensor_tensor(Yc[:, e], Yt[:, e, 256:UPS].unsqueeze(2).to_broadcast([TR, TAIL, IMGS]),
                                      mask[:], ALU.mult).then_inc(e_yc, 1)
                if next_out is not None:
                    stats_out(next_out[0], next_out[1], pair_of(k, 3))
                if batch_o is not None:
                    batch_out(batch_o, pair_of(k, 3))
                if up:
                    for m in range(IMGS):
                        dve.wait_ge(e_l, 4 * q + m + 1)
                        dve.tensor_tensor(Y[:, e, :, :, m], ring[:, pair_of(k, 4 + m), :, 0:UPS], L[:, m % 2],
                                          ALU.max).then_inc(e_s2, 1)
                if down:
                    xq = xb[:, x_par(k, 1), (k - 1) % 4].rearrange("p i w -> p (i w)")
                    dve.wait_ge(p_s4, q)
                    dve.wait_ge(g_ok, q)
                    dve.tensor_tensor(xq, xq, ring[:, pair_of(k, 8), 0, :], ALU.add).then_inc(e_x1, 1)
                    dve.wait_ge(e_x1, q)
                    dve.bn_stats(st2[:, e, :], xq).then_inc(b_bn, 1)
                    dve.wait_ge(b_bn, q)
                    carry(dve, carried[1])
                    dve.bn_aggr(mv2[:], st2[:, e, :]).then_inc(b_mv, 1)
                    dve.wait_ge(b_mv, q)
                    dve.tensor_copy(mvx[:, 0, bass.ds(jq, 1), :].rearrange("p o i -> p (o i)"),
                                    mv2[:, 0:1].to_broadcast([128, IMGS]))
                    dve.scalar_tensor_tensor(out=mvx[:, 1, bass.ds(jq, 1), :].rearrange("p o i -> p (o i)"),
                                             in0=mv2[:, 0:1].to_broadcast([128, IMGS]), scalar=mv2[:, 0:1],
                                             in1=mv2[:, 1:2].to_broadcast([128, IMGS]),
                                             op0=ALU.mult, op1=ALU.add).then_inc(b_x, 1)
                if next_in is not None:
                    stats_in(*next_in)

            def spectra(b):
                for j in range(UNITS6):
                    dve.wait_ge(sp_st[j % 2], 32 * (8 * b + j // 2 + 1))
                    dve.wait_ge(e_p6, UNITS6 * b + j + 1)
                    q_ps = ring[:, pair_of(5, 9 + j), 1, :].rearrange("p (n m) -> p n m", n=4)
                    p_sb = psb[:, j % 2, :].rearrange("p (n m) -> p n m", n=4)
                    n0 = 1 if j == 0 else 0
                    if j == 0:
                        dve.tensor_scalar(sp_out[:, 0, 1, 0, :], q_ps[:, 0, :], rs2[:, 0:1], None, ALU.mult)
                        dve.tensor_copy(sp_out[:, 0, 0, 0, 1:], p_sb[:, 0, 1:])
                        dve.tensor_tensor(sp_out[:, 0, 0, 0, 0:1], p_sb[:, 0, 0:1], rs2[:, 2:3], ALU.add)
                    dve.scalar_tensor_tensor(out=sp_out[:, j % 2, 0, n0:, :], in0=q_ps[:, n0:, :],
                                             scalar=rs2[:, 0:1], in1=p_sb[:, n0:, :], op0=ALU.mult, op1=ALU.add)
                    dve.scalar_tensor_tensor(out=sp_out[:, j % 2, 1, n0:, :], in0=q_ps[:, n0:, :],
                                             scalar=rs2[:, 1:2], in1=p_sb[:, n0:, :], op0=ALU.mult,
                                             op1=ALU.add).then_inc(e_s6, 1)

            def first():
                dve.wait_ge(c_ld, 16 * len(ld_consts))
                dve.tensor_scalar(ut[:], ut[:], 2.0, None, ALU.mult).then_inc(c_up, 1)
                stats_in(0, 0)
                stats_out(0, 0, 0)
                for q in range(4):
                    step(q, q, down=q >= 1, jq=q - 1, next_in=(1, 1) if q == 2 else None,
                         next_out=(1, 1) if q == 3 else None)

            def body(t, jq, s6):
                for k in range(8):
                    nh = (2 * t + 2, 0) if k < 4 else (2 * t + 3, 1)
                    step(8 * t + 4 + k, k + 4, jq=jq(k), next_in=nh if k % 4 == 2 else None,
                         next_out=nh if k % 4 == 3 else None,
                         batch_o=s6 if k == 5 else None)
                    if k == 5 and s6 is not None:
                        spectra(s6)

            def last():
                for k in range(4):
                    step(252 + k, k + 4, jq=27 + k)

            def drain():
                step(NQ, 0, up=False, jq=31)
                step(NQ + 1, 1, up=False, down=False, batch_o=B - 1)
                spectra(B - 1)

            steps(dve, first, body, last, drain)


def phase2(nc, spec, bn_d, bst_d, cst_d, dst_d, am_d, fd):
    with ExitStack() as ctx:
        def sb(name, shape, dt=F32):
            return ctx.enter_context(nc.sbuf_tensor(name, shape, dt))

        b_hi = sb("b_hi", [128, 2, RANK_I, 2, C], F16)
        b_lo = sb("b_lo", [128, RANK_I, 2, C], F16)
        w_st = sb("w_st", [128, 2, MODES, MODES], F16)
        am = sb("am", [128, 2, 2, 2 * C])
        factors(nc, bn_d, bst_d, cst_d, dst_d, am_d, b_hi, b_lo, w_st, am)
        modes(nc, spec, b_hi, b_lo, w_st, am, fd)


def factors(nc, bn_d, bst_d, cst_d, dst_d, am_d, b_hi, b_lo, w_st, am):
    CH = 16
    with ExitStack() as ctx:
        def sb(name, shape, dt=F32):
            return ctx.enter_context(nc.sbuf_tensor(name, shape, dt))

        def sem(name):
            return ctx.enter_context(nc.semaphore(name))

        ps = ctx.enter_context(nc.psum_tensor("ps_w", [128, 8, 512], F32))
        cst = sb("cst", [128, MODES, 4 * RANK_J])
        dst = sb("dst", [128, MODES])
        wf = sb("wf", [128, 2, MODES, MODES])
        stage = sb("stage", [128, 2, CH, 2, C])
        ext = sb("ext", [128, 6])
        top = sb("top", [128, 6])
        mag = sb("mag", [128, 2])
        inv = sb("inv", [128, 2])
        sgn = sb("sgn", [128, 2])
        back = sb("back", [128, 1])

        c_ld = sem("fc_ld")
        s_ld = [sem("fs_ld0"), sem("fs_ld1")]
        f_neg = sem("f_neg")
        f_wp = sem("f_wp")
        f_we = sem("f_we")
        f_bm = [sem("f_bm0"), sem("f_bm1")]
        f_ext = sem("f_ext")
        f_top = sem("f_top")
        k = [sem(f"f_k{n}") for n in range(6)]
        f_w = sem("f_w")
        f_sc = sem("f_sc")
        f_hi = sem("f_hi")
        f_lo = [sem("f_lo0"), sem("f_lo1")]

        consts = ((cst, cst_d), (dst, dst_d), (am, am_d))
        chunks = [(z, c) for z in range(2) for c in range(RANK_I // CH)]
        block = ctx.enter_context(nc.Block())

        @block.sync
        def _(sp):
            for d, src in consts:
                sp.dma_start(d[:], src).then_inc(c_ld, 16)
            for z in range(2):
                sp.dma_start(stage[:, z].rearrange("p i r c -> p (i r c)"), bn_d[z],
                             max_dma_last_dim=4096).then_inc(s_ld[z], 16)
            for n, (z, c) in enumerate(chunks):
                e = n % 2
                if n < 2:
                    sp.wait_ge(f_bm[e], 1)
                else:
                    sp.wait_ge(f_lo[e], n // 2)
                sp.dma_start(stage[:, e], bst_d[z, :, CH * c:CH * c + CH]).then_inc(s_ld[e], 16)

        @block.tensor
        def _(pe):
            pe.wait_ge(f_neg, 1)
            for u in range(16):
                z = u // 8
                r = slice(64 * z, 64 * z + 64)
                if u >= 8:
                    pe.wait_ge(f_we, u - 7)
                for n in range(8):
                    mm = pe.matmul(ps[:, u % 8, 64 * n:64 * n + 64], cst[r, 8 * (u % 8) + n, :], dst[r, :],
                                   start=True, stop=True)
                mm.then_inc(f_wp, 1)

        @block.gpsimd
        def _(pool):
            pool.wait_ge(f_ext, 1)
            pool.partition_all_reduce(top[:], ext[:], 128, bass.bass_isa.ReduceOp.absmax).then_inc(f_top, 1)

        @block.scalar
        def _(act):
            act.wait_ge(f_sc, 1)
            for n, (z, c) in enumerate(chunks):
                e = n % 2
                act.wait_ge(s_ld[e], 16 * (n // 2 + 2))
                for r in range(2):
                    a = act.activation(stage[:, e, :, r, :], stage[:, e, :, r, :], ACT.Copy, scale=sgn[:, r:r + 1])
                a.then_inc(f_hi, 1)
                act.wait_ge(f_hi, 2 * n + 1)
                act.activation(b_hi[:, z, CH * c:CH * c + CH], stage[:, e], ACT.Copy).then_inc(f_hi, 1)

        @block.vector
        def _(dve):
            def flat(t):
                return t.rearrange("p s y -> p (s y)")

            dve.wait_ge(c_ld, 16 * len(consts))
            for t in (32, 96):
                for h in (0, 2 * RANK_J):
                    dve.tensor_scalar(cst[t:t + 32, :, h:h + RANK_J], cst[t:t + 32, :, h:h + RANK_J], -1.0, None,
                                      ALU.mult).then_inc(k[0], 1)
            dve.wait_ge(k[0], 4)
            dve.tensor_scalar(am[64:, :, 0, 0:C], am[64:, :, 0, 0:C], -1.0, None, ALU.mult)
            dve.tensor_scalar(am[0:64, :, 1, 0:C], am[0:64, :, 1, 0:C], -1.0, None, ALU.mult)
            dve.tensor_scalar(am[64:, :, 1, :], am[64:, :, 1, :], -1.0, None, ALU.mult).then_inc(f_neg, 1)
            for z in range(2):
                dve.wait_ge(s_ld[z], 16)
                v = stage[:, z].rearrange("p i r c -> p (i r c)")
                dve.tensor_reduce(ext[:, 2 * z:2 * z + 1], v, AX.X, ALU.max)
                dve.tensor_reduce(ext[:, 2 * z + 1:2 * z + 2], v, AX.X, ALU.min).then_inc(f_bm[z], 1)
            for u in range(16):
                dve.wait_ge(f_wp, u + 1)
                dve.tensor_copy(flat(wf[:, u // 8, 8 * (u % 8):8 * (u % 8) + 8, :]), ps[:, u % 8, :]).then_inc(f_we, 1)
            dve.wait_ge(f_we, 16)
            w_all = wf[:].rearrange("p z s y -> p (z s y)")
            dve.tensor_reduce(ext[:, 4:5], w_all, AX.X, ALU.max)
            dve.tensor_reduce(ext[:, 5:6], w_all, AX.X, ALU.min).then_inc(f_ext, 1)
            dve.wait_ge(f_top, 1)
            dve.tensor_reduce(mag[:, 0:1], top[:, 0:4], AX.X, ALU.max)
            dve.tensor_reduce(mag[:, 1:2], top[:, 4:6], AX.X, ALU.max).then_inc(k[1], 1)
            dve.wait_ge(k[1], 1)
            dve.tensor_scalar(mag[:], mag[:], 1e-30, None, ALU.max).then_inc(k[2], 1)
            dve.wait_ge(k[2], 1)
            dve.reciprocal(inv[:], mag[:]).then_inc(k[3], 1)
            dve.tensor_scalar(back[:], mag[:, 0:1], mag[:, 1:2], X_SCALE, ALU.mult, ALU.mult).then_inc(k[4], 1)
            dve.wait_ge(k[3], 1)
            dve.tensor_copy(sgn[:, 1:2], inv[:, 0:1])
            for t in range(0, 128, 32):
                d = dve.tensor_scalar(sgn[t:t + 32, 0:1], inv[t:t + 32, 0:1], 1.0 if t % 64 == 0 else -1.0, None,
                                      ALU.mult)
            d.then_inc(f_sc, 1)
            dve.wait_ge(k[4], 1)
            dve.tensor_scalar(am[:], am[:], back[:, 0:1], None, ALU.mult)
            dve.tensor_scalar(w_all, w_all, inv[:, 1:2], None, ALU.mult).then_inc(k[5], 1)
            dve.wait_ge(k[5], 1)
            dve.tensor_copy(w_st[:], wf[:]).then_inc(f_w, 1)
            dve.wait_ge(f_w, 1)
            for z in range(2):
                r = slice(64 - 64 * z, 128 - 64 * z)
                dve.tensor_tensor(w_st[r, z], wf[r, z], w_st[r, z], ALU.subtract)
            for n, (z, c) in enumerate(chunks):
                e = n % 2
                r = slice(64 * z, 64 * z + 64)
                dve.wait_ge(f_hi, 2 * n + 2)
                dve.tensor_tensor(b_lo[r, CH * c:CH * c + CH], stage[r, e], b_hi[r, z, CH * c:CH * c + CH],
                                  ALU.subtract).then_inc(f_lo[e], 1)


def modes(nc, spec, b_hi, b_lo, w_st, am, fd):
    with ExitStack() as ctx:
        def sb(name, shape, dt=F32):
            return ctx.enter_context(nc.sbuf_tensor(name, shape, dt))

        def sem(name):
            return ctx.enter_context(nc.semaphore(name))

        ring = ctx.enter_context(nc.psum_tensor("ring2", [128, 4, 2, 512], F32))
        wcur = sb("wcur", [128, 2, 2, MODES], F16)
        Mh = sb("Mh", [128, 2, MODES, 2 * RANK_I], F16)
        Ml = sb("Ml", [128, 2, MODES, 2 * RANK_I], F16)
        xin = sb("xin", [128, 2, B * 2 * MODES])
        xs = sb("xs", [128, 2, 2, B * 2, MODES], F16)
        pout = sb("pout", [128, 2, 2, B, MODES])
        ft = sb("ft", [128, 4, 2, 2, C])
        tmp = sb("tmp", [128, 2, 2, 2 * C])

        x_ld = [sem("xa_ld"), sem("xb_ld")]
        x_hi = [sem("xa_hi"), sem("xb_hi")]
        x_cv = [sem("xa_cv"), sem("xb_cv")]
        w_zero = sem("w_zero")
        w_cur = [sem("wa_cur"), sem("wb_cur")]
        p_bld = sem("p_bld")
        e_hi = sem("e_hi")
        e_lo = sem("e_lo")
        p_app = [sem("p_app0"), sem("p_app1")]
        e_app = [sem("e_app0"), sem("e_app1")]
        p_out = sem("p_out")
        e_out = sem("e_out")
        f_st = [sem("f_st0"), sem("f_st1")]
        k_tmp = sem("k_tmp")
        carried = sem("carried2")

        block = ctx.enter_context(nc.Block())

        @block.sync
        def _(sp):
            def load(s, z):
                sp.dma_start(xin[:, z], spec[bass.ds(64 * z + s, 1)].rearrange("s c b m -> (s c) (b m)")
                             ).then_inc(x_ld[z], 16)

            def store(s, u):
                sp.wait_ge(e_out, 2 * s + u + 1)
                for p in (2 * u, 2 * u + 1):
                    for z in range(2):
                        sp.dma_start(fd[128 * p:128 * p + 128, :, bass.ds(64 * z + s, 1), :]
                                     .rearrange("p r s o -> p r (s o)"), ft[:, p, z]).then_inc(f_st[u], 16)

            for z in range(2):
                load(0, z)
            for z in range(2):
                sp.wait_ge(x_cv[z], 1)
                load(1, z)
            with sp.Fori(1, MODES - 1) as s:
                store(s - 1, 0)
                store(s - 1, 1)
                for z in range(2):
                    sp.wait_ge(x_cv[z], s + 1)
                    load(s + 1, z)
            for s in (MODES - 2, MODES - 1):
                store(s, 0)
                store(s, 1)
            for u in range(2):
                sp.wait_ge(f_st[u], 64 * MODES)

        @block.gpsimd
        def _(pool):
            pool.memset(wcur[:], 0.0).then_inc(w_zero, 1)
            pool.wait_ge(w_zero, 1)

            def current(s, z):
                r = slice(64 * z, 64 * z + 64)
                pool.tensor_copy(wcur[:, z, 0, :], w_st[:, z, bass.ds(s, 1), :].rearrange("p s y -> p (s y)")
                                 ).then_inc(w_cur[z], 1)
                pool.wait_ge(w_cur[z], 2 * s + 1)
                carry(pool, carried)
                pool.tensor_copy(wcur[r, z, 1, :], w_st[r, z, bass.ds(s, 1), :].rearrange("p s y -> p (s y)")
                                 ).then_inc(w_cur[z], 1)
                pool.wait_ge(w_cur[z], 2 * s + 2)

            def convert(s, z):
                pool.wait_ge(x_ld[z], 16 * (s + 1))
                wait(pool, p_app[z], s)
                carry(pool, carried)
                hi = xs[:, z, 0].rearrange("p b y -> p (b y)")
                pool.tensor_copy(hi, xin[:, z]).then_inc(x_hi[z], 1)
                pool.wait_ge(x_hi[z], s + 1)
                pool.tensor_tensor(xs[:, z, 1].rearrange("p b y -> p (b y)"), xin[:, z], hi,
                                   ALU.subtract).then_inc(x_cv[z], 1)
                pool.wait_ge(x_cv[z], s + 1)

            current(0, 0)
            current(0, 1)
            convert(0, 0)
            convert(0, 1)
            with pool.Fori(1, MODES) as s:
                pool.wait_ge(p_bld, 16 * s - 8)
                current(s, 0)
                pool.wait_ge(p_bld, 16 * s)
                current(s, 1)
                convert(s, 0)
                convert(s, 1)
            carry(pool, carried)

        @block.tensor
        def _(pe):
            def build(s, z):
                pe.wait_ge(w_cur[z], 2 * s + 2)
                for u in range(8):
                    if u >= 4:
                        pe.wait_ge(e_lo, 16 * s + 8 * z + u - 3)
                    elif z == 0:
                        wait(pe, e_lo, 16 * s)
                        wait(pe, e_app[0], s)
                    else:
                        pe.wait_ge(e_lo, 16 * s + 8)
                        wait(pe, e_app[1], s)
                        if u >= 2:
                            wait(pe, e_out, 2 * s - 3 + u)
                    pr = (11 * z + u) % 4
                    for n in range(16):
                        m = 16 * u + n
                        o = ring[:, pr, n // 8, 64 * (n % 8):64 * (n % 8) + 64]
                        pe.matmul(o, b_hi[:, z, m % 64, m // 64, :], wcur[:, z, 0, :], start=True, stop=False)
                        mm = pe.matmul(o, b_lo[:, m % 64, m // 64, :], wcur[:, z, 1, :], start=False, stop=True)
                    mm.then_inc(p_bld, 1)

            def apply(s, z, n, last=False):
                pe.wait_ge(e_lo, 16 * s + 8 * z + 8)
                if z == 0:
                    pe.wait_ge(e_lo, 16 * s + 13)
                elif not last:
                    pe.wait_ge(e_lo, 16 * s + 21)
                pe.wait_ge(x_cv[z], s + 1)
                for y in range(MODES):
                    o = ring[:, n % 4, y // 32, 16 * (y % 32):16 * (y % 32) + 16]
                    pe.matmul(o, Mh[:, z, y, :], xs[:, z, 0, :, y], start=True, stop=False)
                    pe.matmul(o, Mh[:, z, y, :], xs[:, z, 1, :, y], start=False, stop=False)
                    mm = pe.matmul(o, Ml[:, z, y, :], xs[:, z, 0, :, y], start=False, stop=True)
                mm.then_inc(p_app[z], 1)

            def out(s, last=False):
                pe.wait_ge(e_app[0], s + 1)
                pe.wait_ge(e_app[1], s + 1)
                if not last:
                    pe.wait_ge(e_lo, 16 * s + 23)
                for u in range(2):
                    for n in range(2):
                        p = 2 * u + n
                        for z in range(2):
                            for r in range(2):
                                mm = pe.matmul(ring[:, (9 + u) % 4, n, 256 * z:256 * z + 256],
                                               pout[:, z, r, 2 * p:2 * p + 2, :].rearrange("p b y -> p (b y)"),
                                               am[:, z, r, :], start=(r == 0), stop=(r == 1))
                    mm.then_inc(p_out, 1)

            build(0, 0)
            build(0, 1)
            apply(0, 0, 19)
            with pe.Fori(1, MODES) as s:
                build(s, 0)
                apply(s - 1, 1, 8)
                out(s - 1)
                build(s, 1)
                apply(s, 0, 19)
            apply(MODES - 1, 1, 8, last=True)
            out(MODES - 1, last=True)

        def unit(z, u):
            return (ring[:, (11 * z + u) % 4].rearrange("c k (m y) -> c (k m) y", y=MODES),
                    Mh[:, z, :, 16 * u:16 * u + 16].rearrange("c y m -> c m y"),
                    Ml[:, z, :, 16 * u:16 * u + 16].rearrange("c y m -> c m y"))

        @block.scalar
        def _(act):
            def build(s, z):
                for u in range(8):
                    act.wait_ge(p_bld, 16 * s + 8 * z + u + 1)
                    ps, hi, _lo = unit(z, u)
                    act.activation(hi, ps, ACT.Copy).then_inc(e_hi, 1)

            def apply(s, z, n):
                act.wait_ge(p_app[z], s + 1)
                act.activation(pout[:, z].rearrange("p r b y -> p y b r"),
                               ring[:, n % 4].rearrange("p k (y b r) -> p (k y) b r", b=B, r=2),
                               ACT.Copy).then_inc(e_app[z], 1)

            build(0, 0)
            build(0, 1)
            apply(0, 0, 19)
            with act.Fori(1, MODES) as s:
                build(s, 0)
                apply(s - 1, 1, 8)
                build(s, 1)
                apply(s, 0, 19)
            apply(MODES - 1, 1, 8)

        @block.vector
        def _(dve):
            def build(s, z):
                for u in range(8):
                    dve.wait_ge(e_hi, 16 * s + 8 * z + u + 1)
                    ps, hi, lo = unit(z, u)
                    dve.tensor_tensor(lo, ps, hi, ALU.subtract).then_inc(e_lo, 1)

            def out(s, alone=False):
                for u in range(2):
                    dve.wait_ge(p_out, 2 * s + u + 1)
                    if not alone:
                        dve.wait_ge(f_st[u], 64 * s)
                    ps = ring[:, (9 + u) % 4]
                    o = ft[:, 2 * u:2 * u + 2].rearrange("p n z r o -> p n z (r o)")
                    if alone:
                        dve.tensor_copy(o.rearrange("p n z m -> p n (z m)"), ps).then_inc(e_out, 1)
                    else:
                        a, b, t = ps[:, :, 0:256], ps[:, :, 256:512], tmp[:, u]
                        dve.tensor_copy(t, b).then_inc(k_tmp, 1)
                        dve.wait_ge(k_tmp, 2 * (s - 1) + u + 1)
                        dve.tensor_tensor(o[:, :, 0, :], a, t, ALU.add)
                        dve.tensor_tensor(o[:, :, 1, 0:C], t[:, :, C:], a[:, :, C:], ALU.subtract)
                        dve.tensor_tensor(o[:, :, 1, C:], a[:, :, 0:C], t[:, :, 0:C], ALU.subtract).then_inc(e_out, 1)

            build(0, 0)
            build(0, 1)
            build(1, 0)
            out(0, alone=True)
            build(1, 1)
            with dve.Fori(2, MODES) as s:
                build(s, 0)
                out(s - 1)
                build(s, 1)
            out(MODES - 1)


def phase3(nc, fd, x1, iy_d, ix_d, out):
    with ExitStack() as ctx:
        def sb(name, shape):
            return ctx.enter_context(nc.sbuf_tensor(name, shape, F32))

        def sem(name):
            return ctx.enter_context(nc.semaphore(name))

        ring = ctx.enter_context(nc.psum_tensor("ring3", [128, 8, 512], F32))
        iy = sb("iy", [128, W])
        ix = sb("ix", [128, H])
        F = sb("F", [128, 2, 128, C])
        zb = sb("zb", [128, 2, IMGS * W])
        xq = sb("xq", [128, 4, HALF * IMGS, W])

        c_ld = sem("c_ld3")
        f_ld = [sem("f_ld0"), sem("f_ld1")]
        r_ld = sem("r_ld")
        p_z = sem("p_z")
        e_z = sem("e_z")
        p_o = sem("p_o")
        e_o = sem("e_o")
        o_st = [sem("o_st0"), sem("o_st1")]

        fd_v = fd.rearrange("(b y) r s o -> b (y r) (s o)", b=B)
        x1_v = x1.rearrange("n h w -> h n w")
        out_v = out.rearrange("b c h w -> h (b c) w")
        block = ctx.enter_context(nc.Block())

        @block.sync
        def _(sp):
            sp.dma_start(iy[:], iy_d).then_inc(c_ld, 16)
            sp.dma_start(ix[:], ix_d).then_inc(c_ld, 16)

            def load_f(b, e):
                sp.dma_start(F[:, e].rearrange("p s o -> p (s o)"),
                             fd_v[bass.ds(b, 1)].rearrange("b p m -> (b p) m"),
                             max_dma_last_dim=16384).then_inc(f_ld[e], 16)

            def load_x(h, e):
                for n in range(2):
                    sp.dma_start(xq[:, e, 8 * n:8 * n + 8, :],
                                 x1_v[:, bass.ds(16 * h + 8 * n, 8), :]).then_inc(r_ld, 16)

            def store(h, e):
                sp.wait_ge(e_o, 4 * (h + 1))
                sp.dma_start(out_v[:, bass.ds(16 * h, 16), :], xq[:, e]).then_inc(o_st[e % 2], 16)

            for e in range(2):
                sp.sem_inc(o_st[e], 16)
            load_f(0, 0)
            load_x(0, 0)
            sp.wait_ge(r_ld, 32)
            load_x(1, 1)
            load_f(1, 1)
            with sp.Fori(0, B // 2 - 1) as b2:
                for b in range(2):
                    for n in range(8):
                        h = 16 * b2 + 8 * b + n
                        sp.wait_ge(r_ld, 32 * (h + 2))
                        sp.wait_ge(o_st[n % 2], 16 * (8 * b2 + 4 * b + n // 2 + 1))
                        load_x(h + 2, (n + 2) % 4)
                        store(h, n % 4)
                    sp.wait_ge(p_z, 32 * (2 * b2 + b + 1))
                    load_f(2 * b2 + b + 2, b)
            for h in range(48, 64):
                if h < 62:
                    sp.wait_ge(r_ld, 32 * (h + 2))
                    sp.wait_ge(o_st[h % 2], 16 * (h // 2 + 1))
                    load_x(h + 2, (h + 2) % 4)
                store(h, h % 4)
            for e in range(2):
                sp.wait_ge(o_st[e], 16 * 33)

        @block.tensor
        def _(pe):
            pe.wait_ge(c_ld, 32)

            def quad(q, k, first):
                if k < 64:
                    if k % 32 == 0:
                        pe.wait_ge(f_ld[k // 32], first)
                    wait(pe, e_z, q - 3)
                    for m in range(IMGS):
                        mm = pe.matmul(ring[:, k % 4, 128 * m:128 * m + 128], F[:, k // 32, :, 4 * (k % 32) + m],
                                       iy[:], start=True, stop=True)
                    mm.then_inc(p_z, 1)

            def final(q, k):
                pe.wait_ge(e_z, q + 1)
                wait(pe, e_o, q - 3)
                pe.matmul(ring[:, 4 + k % 4, :], ix[:], zb[:, k % 2, :], start=True, stop=True).then_inc(p_o, 1)

            def pair(b2, start):
                for k in range(64):
                    quad(64 * b2 + k, k, 16 * (b2 + 1))
                    if not (start and k == 0):
                        final(64 * b2 + k - 1, (k - 1) % 4)

            pair(0, True)
            with pe.Fori(1, B // 2) as b2:
                pair(b2, False)
            final(NQ - 1, 3)

        @block.scalar
        def _(act):
            def quad(q, k):
                act.wait_ge(p_z, q + 1)
                wait(act, p_o, q - 1)
                act.activation(zb[:, k % 2, :], ring[:, k % 4, :], ACT.Copy).then_inc(e_z, 1)

            for k in range(4):
                quad(k, k)
            with act.Fori(1, NQ // 4) as i:
                for k in range(4):
                    quad(4 * i + k, k)

        @block.vector
        def _(dve):
            with dve.Fori(0, NQ // 16) as i:
                for k in range(16):
                    h = 4 * i + k // 4
                    dve.wait_ge(r_ld, 32 * (h + 1))
                    dve.wait_ge(p_o, 16 * i + k + 1)
                    x_ = xq[:, k // 4, 4 * (k % 4):4 * (k % 4) + 4, :].rearrange("p i w -> p (i w)")
                    dve.tensor_tensor(x_, x_, ring[:, 4 + k % 4, :], ALU.add).then_inc(e_o, 1)


def program(nc, x, ut, dt, dtail, mask, dfth, dftw, ones, bn, bst, cst, dst, am, iy, ix, out):
    x1 = nc.dram_tensor("x1", (B * C, H, W), F32, kind="Internal").ap()
    spec = nc.dram_tensor("spec", (128, C, B, 2 * MODES), F32, kind="Internal").ap()
    fd = nc.dram_tensor("fd", (B * MODES, 2, 128, C), F32, kind="Internal").ap()
    phase1(nc, x, ut, dt, dtail, mask, dfth, dftw, ones, x1, spec)
    phase2(nc, spec, bn, bst, cst, dst, am, fd)
    phase3(nc, fd, x1, iy, ix, out)


def layouts(inputs):
    import numpy as np

    f = np.asarray(inputs["L0_conv_f"])
    ut = np.zeros((H, UPS), np.float32)
    dT = np.zeros((UPS, H), np.float32)
    for i in range(H):
        ut[i, 2 * i:2 * i + TAPS] = f
        dT[2 * i:2 * i + TAPS, i] = f[::-1]
    dt = np.concatenate([dT[0:128, 0:LO], dT[128:256, HI0:]], axis=1)
    tail = dT[256:, TL0:]
    dtail = np.zeros((TR, IMGS * TLN + TLN), np.float32)
    mask = np.zeros((TR, TAIL, IMGS), np.float32)
    for m in range(IMGS):
        dtail[m::IMGS, TLN * m:TLN * m + TLN] = tail
        dtail[m::IMGS, IMGS * TLN:] = tail
        mask[m::IMGS, :, m] = 1.0
    n = np.arange(128)
    ang = 2 * np.pi * (np.outer(n, n) % 128) / 128
    cos, sin = np.cos(ang), np.sin(ang)
    dfth = np.concatenate([cos[:, 0:65], sin[:, 1:64]], axis=1)
    cy, sy = cos[:, 0:MODES], sin[:, 0:MODES]
    dftw = np.stack([np.concatenate([cy, -sy], 1), np.concatenate([-sy, -cy], 1)], axis=1)
    wt = np.full((MODES, 1), 2.0 / (H * W))
    wt[0] = 1.0 / (H * W)
    iy = np.stack([wt * cy.T, -wt * sy.T], axis=1).reshape(128, W)
    f32 = lambda a: np.ascontiguousarray(a, dtype=np.float32)

    bst, cst, dst, am = [], [], [], []
    rows = (np.arange(64), np.concatenate([[0], np.arange(63, 0, -1)]))
    for z in range(2):
        a, b, c, d = (np.asarray(inputs[f"L1_conv_{n}{z + 1}"]) for n in "abcd")
        b = b.transpose(3, 2, 0, 1)
        bst.append(np.concatenate([np.stack([b[0], b[1]], axis=2), np.stack([b[1], b[0]], axis=2)] * 2))
        c = c[:, rows[z]].transpose(3, 2, 1, 0)
        cst += [np.concatenate([c[0], c[1]] * 2, axis=2), np.concatenate([c[1], c[0]] * 2, axis=2)]
        dst += [d[:, :, 0, 0], d[:, :, 0, 1]]
        a = a[0].transpose(2, 1, 0)
        ri, ir = np.concatenate([a[0], a[1]], axis=1), np.concatenate([a[1], a[0]], axis=1)
        am.append(np.stack([np.concatenate([ri, ir]), np.concatenate([ir, ri])], axis=1))
    return {
        "x": np.ascontiguousarray(inputs["x"]), "ut": ut, "dt": f32(dt), "dtail": dtail, "mask": mask,
        "dfth": f32(dfth), "dftw": f32(dftw), "ones": np.full((128, 128), 1.0 / 128, np.float32),
        "bn": np.stack([np.asarray(inputs[f"L1_conv_b{z}"]).reshape(128, -1) for z in (1, 2)]),
        "bst": np.stack(bst), "cst": np.ascontiguousarray(np.concatenate(cst)),
        "dst": np.ascontiguousarray(np.concatenate(dst)), "am": np.ascontiguousarray(np.stack(am, axis=1)),
        "iy": f32(iy), "ix": f32(dfth.T),
    }


def kernel(**inputs):
    import concourse.bacc as _bacc
    from concourse import mybir as _mybir
    from concourse.bass_utils import run_bass_kernel_spmd as _run

    nc = _bacc.Bacc("TRN2", target_bir_lowering=False, num_devices=1, dynamic_dma_scratch_size=1024)
    arrays, args = {}, []
    for name, a in layouts(inputs).items():
        arrays[f"in_{name}"] = a
        args.append(nc.dram_tensor(f"in_{name}", a.shape, _mybir.dt.from_np(a.dtype), kind="ExternalInput").ap())
    args.append(nc.dram_tensor("out_0", (B, C, H, W), F32, kind="ExternalOutput").ap())
    program(nc, *args)
    return _run(nc, [arrays], core_ids=[0]).results[0]["out_0"]
```

```python
from contextlib import ExitStack

import concourse.bass as bass
from concourse import mybir

F32 = mybir.dt.float32
F16 = mybir.dt.float16
AX = mybir.AxisListType
ALU = mybir.AluOpType
ACT = mybir.ActivationFunctionType

B, C, H, W = 8, 128, 128, 128
TAPS = 12
UPS = 2 * H + TAPS - 2
TAIL = UPS - 2 * 128
IMGS = 4
QUADS = C // IMGS
NQ = B * QUADS
LO = 64
HI0 = (128 - TAPS + 2) // 2
TL0 = (256 - TAPS + 2) // 2
TLN = H - TL0
TR = IMGS * TAIL
MODES = 64
RANK_I, RANK_J = 64, 32
SLOPE = 0.01
EPS = 1e-5
X_SCALE = 128.0
UNITS6 = 16
HALF = 4
UNIT_PAIR = (0, 1, 2) * 5 + (1,)
AUX = 3
OUT_AFTER = (6, 9)


def wait(eng, sem, n):
    if isinstance(n, int) and n <= 0:
        return
    eng.wait_ge(sem, n)


def carry(eng, carried):
    eng.sem_inc(carried, 1)


def phase1(nc, x, ut_d, dt_d, dtail_d, mask_d, dfth_d, dftw_d, ones_d, x1, spec):
    with ExitStack() as ctx:
        def sb(name, shape, dt_=F32):
            return ctx.enter_context(nc.sbuf_tensor(name, shape, dt_))

        def sem(name):
            return ctx.enter_context(nc.semaphore(name))

        ring = ctx.enter_context(nc.psum_tensor("ring1", [128, 4, 2, 512], F32))
        ut = sb("ut", [128, UPS])
        dt = sb("dt", [128, LO + H - HI0])
        dtail = sb("dtail", [TR, IMGS * TLN + TLN])
        mask = sb("mask", [TR, TAIL, IMGS])
        dfth = sb("dfth", [128, 128])
        dftw = sb("dftw", [128, 2, 128])
        ones = sb("ones", [128, 128])
        xb = sb("xb", [128, 2, HALF, IMGS, W])
        g = sb("g", [128, 2, IMGS, W])
        uth = sb("uth", [128, 2, UPS], F16)
        dth = sb("dth", [128, 2, LO + H - HI0], F16)
        dtailh = sb("dtailh", [TR, 2, IMGS * TLN + TLN], F16)
        A = sb("A", [128, 2, 2, UPS, IMGS], F16)
        Y = sb("Y", [128, 2, 2, 2, UPS, IMGS], F16)
        Yt = sb("Yt", [TR, 2, 2, UPS], F16)
        Yc = sb("Yc", [TR, 2, 2, TAIL, IMGS], F16)
        Yf = sb("Yf", [128, IMGS, 2, UPS])
        Ytf = sb("Ytf", [TR, 2, UPS])
        L = sb("L", [128, 2, 2, UPS])
        Lt = sb("Lt", [TR, UPS])
        Z = sb("Z", [128, 2, 2, 2, IMGS, H], F16)
        Zt = sb("Zt", [TR, 2, 2, H], F16)
        fm = sb("fm", [128, 6])
        fac = sb("fac", [128, 2])
        G = sb("G", [128, C, 128])
        psb = sb("psb", [128, 2, 512])
        sp_out = sb("sp_out", [128, 2, 2, 4, 128])
        st = sb("st", [128, HALF, 6])
        mv = sb("mv", [128, HALF, 2])
        sq = sb("sq", [128, HALF])
        var = sb("var", [128, HALF])
        std = sb("std", [128, HALF])
        rstd = sb("rstd", [128, 2, HALF])
        nmr = sb("nmr", [128, 2, HALF])
        st2 = sb("st2", [128, 2, 6])
        mv2 = sb("mv2", [128, 2])
        mvx = sb("mvx", [128, 2, QUADS, IMGS])
        tot = sb("tot", [128, 2 * HALF])
        tt2 = sb("tt2", [128, 5])
        rs2 = sb("rs2", [128, 3])

        c_ld = sem("c_ld")
        c_up = sem("c_up")
        x_ld = sem("x_ld")
        x1_st = sem("x1_st")
        sp_st = [sem("sp_st0"), sem("sp_st1")]
        g_ok = sem("g_ok")
        p_s1, p_s2, p_s3, p_tl, p_s4, p_s5, p_s6 = [sem(n) for n in ("p_s1", "p_s2", "p_s3", "p_tl", "p_s4", "p_s5", "p_s6")]
        e_s1 = sem("e_s1")
        e_ah = sem("e_ah")
        e_l = sem("e_l")
        e_lt = sem("e_lt")
        e_yf = sem("e_yf")
        e_ytf = sem("e_ytf")
        e_yh = sem("e_yh")
        e_yth = sem("e_yth")
        e_y = sem("e_y")
        e_y3 = sem("e_y3")
        e_zh = sem("e_zh")
        e_zth = sem("e_zth")
        k_f = sem("k_f")
        e_s3 = sem("e_s3")
        e_t2 = sem("e_t2")
        e_yc = sem("e_yc")
        e_t3 = sem("e_t3")
        e_x1 = sem("e_x1")
        e_s5 = sem("e_s5")
        e_p6 = sem("e_p6")
        e_s6 = sem("e_s6")
        p_st = sem("p_st")
        carried = [sem(f"carried_{n}") for n in ("pool", "dve", "sp")]
        p_st2 = sem("p_st2")
        k_bn, k_mv, k_sq, k_e2 = [sem(n) for n in ("k_bn", "k_mv", "k_sq", "k_e2")]
        k_m2, k_var, k_rs, k_nm = [sem(n) for n in ("k_m2", "k_var", "k_rs", "k_nm")]
        b_bn, b_mv, b_x = [sem(n) for n in ("b_bn", "b_mv", "b_x")]
        b_m2, b_var, b_rs, b_dc = [sem(n) for n in ("b_m2", "b_var", "b_rs", "b_dc")]
        b_tot, b_dif, b_sd, k_sd = [sem(n) for n in ("b_tot", "b_dif", "b_sd", "k_sd")]

        x_v = x.rearrange("b c h w -> h (b c) w")
        x1_v = x1.rearrange("n h w -> h n w")
        ld_consts = ((ut, ut_d), (dt, dt_d), (dtail, dtail_d), (mask, mask_d), (dfth, dfth_d), (dftw, dftw_d),
                     (ones, ones_d))

        def pair_of(k, u):
            return (9 * k + u) % 4

        def x_par(k, back):
            return (k - back) // HALF % 2

        def steps(eng, first, body, last, drain):
            first()
            with eng.Fori(0, B - 1) as b:
                with eng.Fori(0, 3) as i:
                    body(4 * b + i, lambda k: 8 * i + 3 + k, None)
                body(4 * b + 3, lambda k: (27 + k) % QUADS, b)
            with eng.Fori(0, 3) as i:
                body(4 * (B - 1) + i, lambda k: 8 * i + 3 + k, None)
            last()
            drain()

        block = ctx.enter_context(nc.Block())

        @block.sync
        def _(sp):
            def load_half(h, par):
                for n in range(2):
                    sp.dma_start(xb[:, par, 2 * n:2 * n + 2].rearrange("p q i w -> p (q i) w"),
                                 x_v[:, bass.ds(16 * h + 8 * n, 8), :]).then_inc(x_ld, 16)

            def turn(h, par, more=True):
                sp.wait_ge(e_x1, 4 * h)
                sp.dma_start(x1_v[:, bass.ds(16 * (h - 1), 16), :],
                             xb[:, par].rearrange("p q i w -> p (q i) w")).then_inc(x1_st, 16)
                if more:
                    sp.wait_ge(p_s5, 4 * h)
                    sp.wait_ge(b_bn, 4 * h)
                    carry(sp, carried[2])
                    sp.wait_ge(x1_st, 16 * h)
                    load_half(h + 1, par)

            def store_spectra(b):
                with sp.Fori(0, UNITS6 // 2) as j2:
                    for e in range(2):
                        j = 2 * j2 + e
                        sp.wait_ge(e_s6, UNITS6 * b + j + 1)
                        for z in range(2):
                            sp.dma_start(spec[bass.ds(64 * z + 4 * j, 4), :, bass.ds(b, 1), :]
                                         .rearrange("s c o m -> c s (o m)"),
                                         sp_out[:, e, z]).then_inc(sp_st[e], 16)

            def first():
                for e in range(2):
                    sp.sem_inc(sp_st[e], 32)
                load_half(0, 0)
                for dst, src in ld_consts:
                    sp.dma_start(dst[:], src).then_inc(c_ld, 16)
                sp.wait_ge(x_ld, 32)
                load_half(1, 1)

            def body(t, jq, s6):
                turn(2 * t + 1, 0)
                turn(2 * t + 2, 1)
                if s6 is not None:
                    store_spectra(s6)

            def drain():
                turn(2 * 32, 1, more=False)
                store_spectra(B - 1)
                sp.wait_ge(x1_st, 16 * 64)
                for e in range(2):
                    sp.wait_ge(sp_st[e], 32 + 2 * 16 * B * UNITS6 // 2)

            steps(sp, first, body, lambda: turn(63, 0, more=False), drain)

        @block.gpsimd
        def _(pool):
            def low(q, e):
                for m in range(IMGS - 1):
                    pool.wait_ge(e_yh, 4 * q + m + 1)
                    pool.tensor_tensor(Y[:, e, 1, :, :, m], Yf[:, m], Y[:, e, 0, :, :, m],
                                       ALU.subtract).then_inc(e_y, 1)
                    pool.wait_ge(e_y, 3 * q + m + 1)
                pool.wait_ge(e_t2, q + 1)
                for v in range(2):
                    pool.tensor_tensor(Yc[:, e, v], Yt[:, e, v, 256:UPS].unsqueeze(2).to_broadcast([TR, TAIL, IMGS]),
                                       mask[:], ALU.mult).then_inc(e_yc, 1)
                    pool.wait_ge(e_yc, 2 * q + v + 1)

            def half(h, par):
                for e in range(HALF):
                    q = 4 * h + e
                    if e == 0:
                        pool.wait_ge(k_nm, h + 1)
                    wait(pool, p_s1, 2 * (q - 1))
                    carry(pool, carried[0])
                    pool.tensor_scalar(g[:, e % 2].rearrange("p i w -> p (i w)"),
                                       xb[:, par, e].rearrange("p i w -> p (i w)"),
                                       rstd[:, par, e:e + 1], nmr[:, par, e:e + 1],
                                       ALU.mult, ALU.add).then_inc(g_ok, 1)
                    pool.wait_ge(g_ok, q + 1)
                    if not isinstance(q, int) or q >= 1:
                        low(q - 1, (e - 1) % 2)

            def body(t, jq, s6):
                half(2 * t + 1, 1)
                half(2 * t + 2, 0)

            pool.wait_ge(c_ld, 16 * len(ld_consts))
            steps(pool, lambda: half(0, 0), body, lambda: half(63, 1), lambda: low(NQ - 1, 1))

        @block.tensor
        def _(pe):
            def pairs(out, data, const, start=False, stop=False):
                for n, (v, c) in enumerate(((0, 0), (0, 1), (1, 0))):
                    mm = pe.matmul(out, data(v), const(c), start=(start and n == 0), stop=(stop and n == 2),
                                   skip_group_check=True)
                return mm

            def step(q, k, up=True, down=True, rows=True, next_half=None, batch=None):
                e = k % 2
                if up:
                    pe.wait_ge(g_ok, q + 1)
                    for n in range(2):
                        wait(pe, e_yf, 4 * (q - 1) + 2 + n)
                        for m in range(2):
                            mm = pe.matmul(ring[:, pair_of(k, n), m, 0:UPS], g[:, e, 2 * n + m, :], ut[:],
                                           start=True, stop=True)
                        mm.then_inc(p_s1, 1)
                if down:
                    o = 1 - e
                    pe.wait_ge(e_yf, 4 * q)
                    for m in (0, 1, 3, 2):
                        if m < 3:
                            pe.wait_ge(e_y, 3 * q - 2 + m)
                        else:
                            pe.wait_ge(e_y3, q)
                        for wt in range(2):
                            bank = ring[:, pair_of(k, 2), wt, :]
                            pairs(bank[:, 128 * m:128 * m + LO],
                                  lambda v: Y[:, o, v, 0, 128 * wt:128 * wt + 128, m],
                                  lambda v: dth[:, v, 0:LO], start=(m == 0))
                            pairs(bank[:, 128 * m + HI0:128 * m + 128],
                                  lambda v: Y[:, o, v, 1, 128 * wt:128 * wt + 128, m], lambda v: dth[:, v, LO:])
                    pe.wait_ge(e_t2, q)
                    for wt in range(2):
                        bank = ring[:, pair_of(k, 2), wt, :]
                        mm = pairs(bank.rearrange("p (i h) -> p i h", i=IMGS)[:, :, TL0:H],
                                   lambda v: Yt[:, o, v, 128 * wt:128 * wt + 128],
                                   lambda v: dtailh[:, v, 0:IMGS * TLN], stop=True)
                    mm.then_inc(p_s3, 1)
                tl = pair_of(k, 3)
                wait(pe, e_x1, q - 1)
                wait(pe, e_s5, q - 2)
                if next_half is not None:
                    pe.wait_ge(k_e2, next_half + 1)
                    pe.matmul(ring[:, tl, 1, 400:400 + 2 * HALF], ones[:], mv[:].rearrange("p q s -> p (q s)"),
                              start=True, stop=True).then_inc(p_st, 1)
                if batch is not None:
                    pe.wait_ge(b_x, QUADS * (batch + 1))
                    for s in range(2):
                        mm = pe.matmul(ring[:, tl, 1, 500 + s:501 + s], mvx[:, s].rearrange("p q i -> p (q i)"),
                                       ones[:, 0:1], start=True, stop=True)
                    mm.then_inc(p_st2, 1)
                if down:
                    pe.wait_ge(e_yc, 2 * q)
                    zt = ring[0:TR, tl, 0, 0:H]
                    pairs(zt[:, 0:LO], lambda v: Y[:, o, v, 0, 256:UPS, :].rearrange("p t i -> p (t i)"),
                          lambda v: dth[:, v, 0:LO], start=True)
                    pairs(zt[:, HI0:H], lambda v: Y[:, o, v, 1, 256:UPS, :].rearrange("p t i -> p (t i)"),
                          lambda v: dth[:, v, LO:])
                    mm = pairs(zt[:, TL0:H], lambda v: Yc[:, o, v].rearrange("p t i -> p (t i)"),
                               lambda v: dtailh[:, v, IMGS * TLN:], stop=True)
                if up:
                    pe.wait_ge(e_s1, 2 * q + 2)
                    mm = pairs(ring[0:TR, tl, 1, 0:UPS],
                               lambda v: A[:, e, v, 256:UPS, :].rearrange("p t i -> p (t i)"),
                               lambda v: uth[:, v, :], start=True, stop=True)
                if up or down:
                    mm.then_inc(p_tl, 1)
                if up:
                    for m in range(IMGS):
                        pr = pair_of(k, 4 + m)
                        if m == 2 and down:
                            pe.wait_ge(e_s3, q)
                        if m == 3:
                            pe.wait_ge(e_ytf, q + 1)
                            wait(pe, e_t3, q)
                            if next_half is not None:
                                pe.wait_ge(k_nm, next_half + 1)
                            if batch is not None:
                                pe.wait_ge(b_tot, batch + 1)
                        for t in range(2):
                            mm = pairs(ring[:, pr, t, 0:UPS], lambda v: A[:, e, v, 128 * t:128 * t + 128, m],
                                       lambda v: uth[:, v, :], start=True, stop=True)
                        mm.then_inc(p_s2, 1)
                pr = pair_of(k, 8)
                if up:
                    pe.wait_ge(e_yf, 4 * q + 1)
                if down:
                    pe.wait_ge(e_s3, q)
                    pe.wait_ge(e_t3, q)
                    bank = ring[:, pr, 0, :]
                    for m in range(IMGS):
                        pairs(bank[:, 128 * m:128 * m + LO], lambda v: Z[:, o, v, 0, m, :],
                              lambda v: dth[:, v, 0:LO], start=(m == 0))
                        pairs(bank[:, 128 * m + HI0:128 * m + 128], lambda v: Z[:, o, v, 1, m, :],
                              lambda v: dth[:, v, LO:])
                    pairs(bank.rearrange("p (i w) -> p i w", i=IMGS)[:, :, TL0:W], lambda v: Zt[:, o, v, :],
                          lambda v: dtailh[:, v, 0:IMGS * TLN], stop=True).then_inc(p_s4, 1)
                if rows:
                    pe.wait_ge(e_x1, q - 1)
                    for m in range(IMGS):
                        mm = pe.matmul(ring[:, pr, 1, 128 * m:128 * m + 128],
                                       xb[:, x_par(k, 2), (k - 2) % 4, m, :], dfth[:], start=True, stop=True)
                    mm.then_inc(p_s5, 1)

            def spectra(b):
                pe.wait_ge(e_s5, QUADS * (b + 1))
                for j in range(UNITS6):
                    pr = pair_of(5, 9 + j)
                    if j >= 4:
                        pe.wait_ge(e_s6, UNITS6 * b + j - 3)
                    for n in range(4):
                        s = 4 * j + n
                        pe.matmul(ring[:, pr, 0, 128 * n:128 * n + 128], G[:, :, s], dftw[:, 0, :],
                                  start=True, stop=True)
                        mm = pe.matmul(ring[:, pr, 1, 128 * n:128 * n + 128], G[:, :, 64 + s],
                                       dftw[:, 0 if s == 0 else 1, :], start=True, stop=True)
                    mm.then_inc(p_s6, 1)

            def drained(q, up):
                if up:
                    pe.wait_ge(e_yf, 4 * q + 4)
                pe.wait_ge(e_x1, min(q, NQ) if isinstance(q, int) else q)
                pe.wait_ge(e_s5, q - 1)

            def first():
                pe.wait_ge(c_ld, 16 * len(ld_consts))
                pe.wait_ge(c_up, 1)
                pe.wait_ge(k_e2, 1)
                pe.matmul(ring[:, 0, 1, 400:400 + 2 * HALF], ones[:], mv[:].rearrange("p q s -> p (q s)"),
                          start=True, stop=True).then_inc(p_st, 1)
                pe.wait_ge(k_nm, 1)
                for q in range(4):
                    step(q, q, down=q >= 1, rows=q >= 2, next_half=1 if q == 3 else None)

            def body(t, jq, s6):
                for k in range(8):
                    q = 8 * t + 4 + k
                    step(q, k + 4, next_half=2 * t + 2 if k == 3 else 2 * t + 3 if k == 7 else None,
                         batch=s6 if k == 5 else None)
                    if k == 5 and s6 is not None:
                        drained(q, True)
                        spectra(s6)
                        pe.wait_ge(e_s6, UNITS6 * (s6 + 1))

            def last():
                for k in range(4):
                    step(4 * 63 + k, k + 4)

            def drain():
                step(NQ, 0, up=False)
                step(NQ + 1, 1, up=False, down=False, batch=B - 1)
                drained(NQ + 1, False)
                spectra(B - 1)

            steps(pe, first, body, last, drain)

        @block.scalar
        def _(act):
            def root(h):
                act.wait_ge(k_var, h + 1)
                act.activation(std[:], var[:], ACT.Sqrt).then_inc(k_sd, 1)

            def step(q, k, up=True, down=True, rows=True, j5=None, next_half=None, batch=None):
                e, o = k % 2, 1 - k % 2
                if up:
                    for n in range(2):
                        act.wait_ge(p_s1, 2 * q + n + 1)
                        act.activation(A[:, e, 0, :, 2 * n:2 * n + 2].rearrange("p h i -> p i h"),
                                       ring[:, pair_of(k, n), :, 0:UPS], ACT.Copy).then_inc(e_ah, 1)
                if down:
                    act.wait_ge(p_s3, q)
                    act.activation(Z[:, o, 0].rearrange("p t i h -> p t (i h)"), ring[:, pair_of(k, 2), :, :],
                                   ACT.Copy).then_inc(e_zh, 1)
                if up:
                    act.wait_ge(p_tl, q + 1)
                    act.activation(Lt[:], ring[0:TR, pair_of(k, 3), 1, 0:UPS], ACT.Copy,
                                   scale=SLOPE).then_inc(e_lt, 1)
                if down:
                    act.wait_ge(p_tl, q + 1)
                    act.activation(Zt[:, o, 0, :], ring[0:TR, pair_of(k, 3), 0, 0:H], ACT.Copy).then_inc(e_zth, 1)
                if next_half is not None:
                    root(next_half)
                if batch is not None:
                    act.wait_ge(b_var, batch + 1)
                    act.activation(tt2[:, 4:5], tt2[:, 3:4], ACT.Sqrt, scale=X_SCALE ** 2).then_inc(b_sd, 1)
                if up:
                    def scaled(m):
                        act.wait_ge(p_s2, 4 * q + m + 1)
                        wait(act, e_yf, 4 * q + m - 1)
                        act.activation(L[:, m % 2], ring[:, pair_of(k, 4 + m), :, 0:UPS], ACT.Copy,
                                       scale=SLOPE).then_inc(e_l, 1)

                    def high(m):
                        act.wait_ge(e_yf, 4 * q + m + 1)
                        act.activation(Y[:, e, 0, :, :, m], Yf[:, m], ACT.Copy).then_inc(e_yh, 1)

                    scaled(0)
                    act.wait_ge(e_ytf, q + 1)
                    act.activation(Yt[:, e, 0, :], Ytf[:, e, :], ACT.Copy).then_inc(e_yth, 1)
                    scaled(1)
                    high(0)
                    scaled(2)
                    high(1)
                    scaled(3)
                    high(2)
                    high(3)
                if rows:
                    act.wait_ge(p_s5, q - 1)
                    act.activation(G[:, bass.ds(4 * j5, IMGS), :],
                                   ring[:, pair_of(k, 8), 1, :].rearrange("p (i s) -> p i s", i=IMGS),
                                   ACT.Copy).then_inc(e_s5, 1)

            def spectra(b):
                act.wait_ge(b_dc, b + 1)
                for j in range(UNITS6):
                    act.wait_ge(p_s6, UNITS6 * b + j + 1)
                    if j >= 2:
                        act.wait_ge(e_s6, UNITS6 * b + j - 1)
                    act.activation(psb[:, j % 2, :], ring[:, pair_of(5, 9 + j), 0, :], ACT.Copy,
                                   scale=rs2[:, 0:1]).then_inc(e_p6, 1)

            def first():
                root(0)
                for q in range(4):
                    step(q, q, down=q >= 1, rows=q >= 2, j5=q - 2, next_half=1 if q == 3 else None)

            def body(t, jq, s6):
                for k in range(8):
                    j5 = jq(k) - 1 if s6 is None else (jq(k) - 1) % QUADS
                    step(8 * t + 4 + k, k + 4, j5=j5,
                         next_half=2 * t + 2 if k == 3 else 2 * t + 3 if k == 7 else None,
                         batch=s6 if k == 5 else None)
                    if k == 5 and s6 is not None:
                        spectra(s6)

            def last():
                for k in range(4):
                    step(252 + k, k + 4, j5=26 + k)

            def drain():
                step(NQ, 0, up=False, j5=30)
                step(NQ + 1, 1, up=False, down=False, j5=31, batch=B - 1)
                spectra(B - 1)

            steps(act, first, body, last, drain)

        @block.vector
        def _(dve):
            def stats_in(h, par):
                dve.wait_ge(x_ld, 32 * (h + 1))
                for n in range(HALF):
                    bn = dve.bn_stats(st[:, n, :], xb[:, par, n].rearrange("p i w -> p (i w)"))
                bn.then_inc(k_bn, 1)
                dve.wait_ge(k_bn, h + 1)
                wait(dve, p_st, h)
                carry(dve, carried[1])
                for n in range(HALF):
                    bn = dve.bn_aggr(mv[:, n, :], st[:, n, :])
                bn.then_inc(k_mv, 1)
                dve.wait_ge(k_mv, h + 1)
                dve.tensor_tensor(sq[:], mv[:, :, 0], mv[:, :, 0], ALU.mult).then_inc(k_sq, 1)
                dve.wait_ge(k_sq, h + 1)
                dve.tensor_tensor(mv[:, :, 1], mv[:, :, 1], sq[:], ALU.add).then_inc(k_e2, 1)

            def stats_out(h, par, pr):
                dve.wait_ge(p_st, h + 1)
                s = ring[:, pr, 1, 400:400 + 2 * HALF].rearrange("p (q s) -> p q s", s=2)
                dve.tensor_copy(tot[:], ring[:, pr, 1, 400:400 + 2 * HALF]).then_inc(k_m2, 1)
                s = tot[:].rearrange("p (q s) -> p q s", s=2)
                dve.wait_ge(k_m2, 3 * h + 1)
                dve.tensor_tensor(sq[:], s[:, :, 0], s[:, :, 0], ALU.mult).then_inc(k_m2, 1)
                dve.wait_ge(k_m2, 3 * h + 2)
                dve.tensor_tensor(var[:], s[:, :, 1], sq[:], ALU.subtract).then_inc(k_m2, 1)
                dve.wait_ge(k_m2, 3 * h + 3)
                dve.tensor_scalar(var[:], var[:], 0.0, EPS, ALU.max, ALU.add).then_inc(k_var, 1)
                dve.wait_ge(k_sd, h + 1)
                if not isinstance(h, int) or h >= 2:
                    dve.wait_ge(g_ok, 4 * (h - 1))
                dve.reciprocal(rstd[:, par, :], std[:]).then_inc(k_rs, 1)
                dve.wait_ge(k_rs, h + 1)
                dve.scalar_tensor_tensor(out=nmr[:, par, :], in0=s[:, :, 0], scalar=-1.0, in1=rstd[:, par, :],
                                         op0=ALU.mult, op1=ALU.mult).then_inc(k_nm, 1)

            def batch_out(b, pr):
                dve.wait_ge(p_st2, b + 1)
                dve.tensor_copy(tt2[:, 0:2], ring[:, pr, 1, 500:502]).then_inc(b_tot, 1)
                dve.wait_ge(b_tot, b + 1)
                dve.tensor_tensor(tt2[:, 2:3], tt2[:, 0:1], tt2[:, 0:1], ALU.mult).then_inc(b_m2, 1)
                dve.wait_ge(b_m2, b + 1)
                dve.tensor_tensor(tt2[:, 3:4], tt2[:, 1:2], tt2[:, 2:3], ALU.subtract).then_inc(b_dif, 1)
                dve.wait_ge(b_dif, b + 1)
                dve.tensor_scalar(tt2[:, 3:4], tt2[:, 3:4], 0.0, EPS, ALU.max, ALU.add).then_inc(b_var, 1)
                dve.wait_ge(b_sd, b + 1)
                dve.reciprocal(rs2[:, 0:1], tt2[:, 4:5]).then_inc(b_rs, 1)
                dve.wait_ge(b_rs, b + 1)
                dve.tensor_scalar(rs2[:, 1:2], rs2[:, 0:1], -1.0, None, ALU.mult)
                dve.scalar_tensor_tensor(out=rs2[:, 2:3], in0=tt2[:, 0:1], scalar=-float(H * W),
                                         in1=rs2[:, 0:1], op0=ALU.mult, op1=ALU.mult).then_inc(b_dc, 1)
                dve.wait_ge(b_dc, b + 1)

            def step(q, k, up=True, down=True, rows=True, j5=None, next_in=None, next_out=None, batch_o=None):
                e, o = k % 2, 1 - k % 2
                if up:
                    for n in range(2):
                        dve.wait_ge(e_ah, 2 * q + n + 1)
                        dve.tensor_tensor(A[:, e, 1, :, 2 * n:2 * n + 2].rearrange("p h i -> p i h"),
                                          ring[:, pair_of(k, n), :, 0:UPS],
                                          A[:, e, 0, :, 2 * n:2 * n + 2].rearrange("p h i -> p i h"),
                                          ALU.subtract).then_inc(e_s1, 1)
                def spread():
                    dve.wait_ge(b_bn, q - 1)
                    carry(dve, carried[1])
                    dve.bn_aggr(mv2[:], st2[:, e, :]).then_inc(b_mv, 1)
                    dve.wait_ge(b_mv, q - 1)
                    dve.tensor_copy(mvx[:, 0, bass.ds(j5, 1), :].rearrange("p o i -> p (o i)"),
                                    mv2[:, 0:1].to_broadcast([128, IMGS]))
                    dve.scalar_tensor_tensor(out=mvx[:, 1, bass.ds(j5, 1), :].rearrange("p o i -> p (o i)"),
                                             in0=mv2[:, 0:1].to_broadcast([128, IMGS]), scalar=mv2[:, 0:1],
                                             in1=mv2[:, 1:2].to_broadcast([128, IMGS]),
                                             op0=ALU.mult, op1=ALU.add).then_inc(b_x, 1)

                if rows:
                    xq = xb[:, x_par(k, 2), (k - 2) % 4].rearrange("p i w -> p (i w)")
                    dve.wait_ge(e_x1, q - 1)
                    dve.bn_stats(st2[:, e, :], xq).then_inc(b_bn, 1)
                    if batch_o is not None or not up:
                        spread()
                if down:
                    dve.wait_ge(e_zh, q)
                    dve.tensor_tensor(Z[:, o, 1].rearrange("p t i h -> p t (i h)"), ring[:, pair_of(k, 2), :, :],
                                      Z[:, o, 0].rearrange("p t i h -> p t (i h)"), ALU.subtract).then_inc(e_s3, 1)
                if up:
                    dve.wait_ge(e_lt, q + 1)
                    wait(dve, e_yth, q - 1)
                    wait(dve, e_t2, q - 1)
                    dve.tensor_tensor(Ytf[:, e, :], ring[0:TR, pair_of(k, 3), 1, 0:UPS], Lt[:],
                                      ALU.max).then_inc(e_ytf, 1)
                if down:
                    dve.wait_ge(e_zth, q)
                    dve.tensor_tensor(Zt[:, o, 1, :], ring[0:TR, pair_of(k, 3), 0, 0:H], Zt[:, o, 0, :],
                                      ALU.subtract).then_inc(e_t3, 1)
                if next_out is not None:
                    stats_out(next_out[0], next_out[1], pair_of(k, 3))
                if batch_o is not None:
                    batch_out(batch_o, pair_of(k, 3))
                if up:
                    for m in range(IMGS):
                        dve.wait_ge(e_l, 4 * q + m + 1)
                        wait(dve, e_y if m < 3 else e_y3, 3 * (q - 1) + m + 1 if m < 3 else q)
                        dve.tensor_tensor(Yf[:, m], ring[:, pair_of(k, 4 + m), :, 0:UPS], L[:, m % 2],
                                          ALU.max).then_inc(e_yf, 1)
                        if m == 1 and rows and batch_o is None:
                            spread()
                        if m == 0:
                            dve.wait_ge(e_yth, q + 1)
                            dve.tensor_tensor(Yt[:, e, 1, :], Ytf[:, e, :], Yt[:, e, 0, :],
                                              ALU.subtract).then_inc(e_t2, 1)
                if down:
                    xq = xb[:, x_par(k, 1), (k - 1) % 4].rearrange("p i w -> p (i w)")
                    dve.wait_ge(p_s4, q)
                    dve.wait_ge(g_ok, q)
                    dve.scalar_tensor_tensor(out=xq, in0=ring[:, pair_of(k, 8), 0, :], scalar=fac[:, 1:2], in1=xq,
                                             op0=ALU.mult, op1=ALU.add).then_inc(e_x1, 1)
                if up:
                    dve.wait_ge(e_yh, 4 * q + IMGS)
                    dve.tensor_tensor(Y[:, e, 1, :, :, IMGS - 1], Yf[:, IMGS - 1], Y[:, e, 0, :, :, IMGS - 1],
                                      ALU.subtract).then_inc(e_y3, 1)
                if next_in is not None:
                    stats_in(*next_in)

            def spectra(b):
                for j in range(UNITS6):
                    dve.wait_ge(sp_st[j % 2], 32 * (8 * b + j // 2 + 1))
                    dve.wait_ge(e_p6, UNITS6 * b + j + 1)
                    q_ps = ring[:, pair_of(5, 9 + j), 1, :].rearrange("p (n m) -> p n m", n=4)
                    p_sb = psb[:, j % 2, :].rearrange("p (n m) -> p n m", n=4)
                    n0 = 1 if j == 0 else 0
                    if j == 0:
                        dve.tensor_scalar(sp_out[:, 0, 1, 0, :], q_ps[:, 0, :], rs2[:, 0:1], None, ALU.mult)
                        dve.tensor_copy(sp_out[:, 0, 0, 0, 1:], p_sb[:, 0, 1:])
                        dve.tensor_tensor(sp_out[:, 0, 0, 0, 0:1], p_sb[:, 0, 0:1], rs2[:, 2:3], ALU.add)
                    dve.scalar_tensor_tensor(out=sp_out[:, j % 2, 0, n0:, :], in0=q_ps[:, n0:, :],
                                             scalar=rs2[:, 0:1], in1=p_sb[:, n0:, :], op0=ALU.mult, op1=ALU.add)
                    dve.scalar_tensor_tensor(out=sp_out[:, j % 2, 1, n0:, :], in0=q_ps[:, n0:, :],
                                             scalar=rs2[:, 1:2], in1=p_sb[:, n0:, :], op0=ALU.mult,
                                             op1=ALU.add).then_inc(e_s6, 1)

            def first():
                dve.wait_ge(c_ld, 16 * len(ld_consts))
                dve.tensor_reduce(fm[:, 0:1], ut[:], AX.X, ALU.max)
                dve.tensor_reduce(fm[:, 1:2], ut[:], AX.X, ALU.min).then_inc(k_f, 1)
                dve.wait_ge(k_f, 1)
                dve.tensor_scalar(fm[:, 2:3], fm[:, 1:2], -1.0, 1e-30, ALU.mult, ALU.max).then_inc(k_f, 1)
                dve.wait_ge(k_f, 2)
                dve.tensor_tensor(fm[:, 3:4], fm[:, 2:3], fm[:, 0:1], ALU.max).then_inc(k_f, 1)
                dve.wait_ge(k_f, 3)
                dve.reciprocal(fm[:, 4:5], fm[:, 3:4])
                dve.tensor_scalar(fac[:, 0:1], fm[:, 3:4], fm[:, 3:4], 2.0, ALU.mult, ALU.mult).then_inc(k_f, 1)
                dve.wait_ge(k_f, 4)
                dve.tensor_tensor(fac[:, 1:2], fac[:, 0:1], fac[:, 0:1], ALU.mult)
                for t, n in ((ut, 128), (dt, 128), (dtail, TR)):
                    v = dve.tensor_scalar(t[:], t[:], fm[0:n, 4:5], None, ALU.mult)
                v.then_inc(k_f, 1)
                dve.wait_ge(k_f, 5)
                for t, h_ in ((ut, uth), (dt, dth), (dtail, dtailh)):
                    v = dve.tensor_copy(h_[:, 0, :], t[:])
                v.then_inc(k_f, 1)
                dve.wait_ge(k_f, 6)
                for t, h_ in ((ut, uth), (dt, dth), (dtail, dtailh)):
                    v = dve.tensor_tensor(h_[:, 1, :], t[:], h_[:, 0, :], ALU.subtract)
                v.then_inc(c_up, 1)
                stats_in(0, 0)
                stats_out(0, 0, 0)
                for q in range(4):
                    step(q, q, down=q >= 1, rows=q >= 2, j5=q - 2, next_in=(1, 1) if q == 2 else None,
                         next_out=(1, 1) if q == 3 else None)

            def body(t, jq, s6):
                for k in range(8):
                    nh = (2 * t + 2, 0) if k < 4 else (2 * t + 3, 1)
                    j5 = jq(k) - 1 if s6 is None else (jq(k) - 1) % QUADS
                    step(8 * t + 4 + k, k + 4, j5=j5, next_in=nh if k % 4 == 2 else None,
                         next_out=nh if k % 4 == 3 else None,
                         batch_o=s6 if k == 5 else None)
                    if k == 5 and s6 is not None:
                        spectra(s6)

            def last():
                for k in range(4):
                    step(252 + k, k + 4, j5=26 + k)

            def drain():
                step(NQ, 0, up=False, j5=30)
                step(NQ + 1, 1, up=False, down=False, j5=31, batch_o=B - 1)
                spectra(B - 1)

            steps(dve, first, body, last, drain)


def phase2(nc, spec, bn_d, bst_d, cst_d, dst_d, am_d, fd):
    with ExitStack() as ctx:
        def sb(name, shape, dt=F32):
            return ctx.enter_context(nc.sbuf_tensor(name, shape, dt))

        b_hi = sb("b_hi", [128, 2, RANK_I, 2, C], F16)
        b_lo = sb("b_lo", [128, RANK_I, 2, C], F16)
        w_st = sb("w_st", [128, 2, MODES, MODES], F16)
        am = sb("am", [128, 2, 2, 2 * C])
        factors(nc, bn_d, bst_d, cst_d, dst_d, am_d, b_hi, b_lo, w_st, am)
        modes(nc, spec, b_hi, b_lo, w_st, am, fd)


def factors(nc, bn_d, bst_d, cst_d, dst_d, am_d, b_hi, b_lo, w_st, am):
    CH = 16
    with ExitStack() as ctx:
        def sb(name, shape, dt=F32):
            return ctx.enter_context(nc.sbuf_tensor(name, shape, dt))

        def sem(name):
            return ctx.enter_context(nc.semaphore(name))

        ps = ctx.enter_context(nc.psum_tensor("ps_w", [128, 8, 512], F32))
        cst = sb("cst", [128, MODES, 4 * RANK_J])
        dst = sb("dst", [128, MODES])
        wf = sb("wf", [128, 2, MODES, MODES])
        stage = sb("stage", [128, 2, CH, 2, C])
        ext = sb("ext", [128, 6])
        top = sb("top", [128, 6])
        mag = sb("mag", [128, 2])
        inv = sb("inv", [128, 2])
        sgn = sb("sgn", [128, 2])
        back = sb("back", [128, 1])

        c_ld = sem("fc_ld")
        s_ld = [sem("fs_ld0"), sem("fs_ld1")]
        f_neg = sem("f_neg")
        f_wp = sem("f_wp")
        f_we = sem("f_we")
        f_bm = [sem("f_bm0"), sem("f_bm1")]
        f_ext = sem("f_ext")
        f_top = sem("f_top")
        k = [sem(f"f_k{n}") for n in range(6)]
        f_w = sem("f_w")
        f_sc = sem("f_sc")
        f_hi = sem("f_hi")
        f_lo = [sem("f_lo0"), sem("f_lo1")]

        consts = ((cst, cst_d), (dst, dst_d), (am, am_d))
        chunks = [(z, c) for z in range(2) for c in range(RANK_I // CH)]
        block = ctx.enter_context(nc.Block())

        @block.sync
        def _(sp):
            for d, src in consts:
                sp.dma_start(d[:], src).then_inc(c_ld, 16)
            for z in range(2):
                sp.dma_start(stage[:, z].rearrange("p i r c -> p (i r c)"), bn_d[z],
                             max_dma_last_dim=4096).then_inc(s_ld[z], 16)
            for n, (z, c) in enumerate(chunks):
                e = n % 2
                if n < 2:
                    sp.wait_ge(f_bm[e], 1)
                else:
                    sp.wait_ge(f_lo[e], n // 2)
                sp.dma_start(stage[:, e], bst_d[z, :, CH * c:CH * c + CH]).then_inc(s_ld[e], 16)

        @block.tensor
        def _(pe):
            pe.wait_ge(f_neg, 1)
            for u in range(16):
                z = u // 8
                r = slice(64 * z, 64 * z + 64)
                if u >= 8:
                    pe.wait_ge(f_we, u - 7)
                for n in range(8):
                    mm = pe.matmul(ps[:, u % 8, 64 * n:64 * n + 64], cst[r, 8 * (u % 8) + n, :], dst[r, :],
                                   start=True, stop=True)
                mm.then_inc(f_wp, 1)

        @block.gpsimd
        def _(pool):
            pool.wait_ge(f_ext, 1)
            pool.partition_all_reduce(top[:], ext[:], 128, bass.bass_isa.ReduceOp.absmax).then_inc(f_top, 1)

        @block.scalar
        def _(act):
            act.wait_ge(f_sc, 1)
            for n, (z, c) in enumerate(chunks):
                e = n % 2
                act.wait_ge(s_ld[e], 16 * (n // 2 + 2))
                for r in range(2):
                    a = act.activation(stage[:, e, :, r, :], stage[:, e, :, r, :], ACT.Copy, scale=sgn[:, r:r + 1])
                a.then_inc(f_hi, 1)
                act.wait_ge(f_hi, 2 * n + 1)
                act.activation(b_hi[:, z, CH * c:CH * c + CH], stage[:, e], ACT.Copy).then_inc(f_hi, 1)

        @block.vector
        def _(dve):
            def flat(t):
                return t.rearrange("p s y -> p (s y)")

            dve.wait_ge(c_ld, 16 * len(consts))
            for t in (32, 96):
                for h in (0, 2 * RANK_J):
                    dve.tensor_scalar(cst[t:t + 32, :, h:h + RANK_J], cst[t:t + 32, :, h:h + RANK_J], -1.0, None,
                                      ALU.mult).then_inc(k[0], 1)
            dve.wait_ge(k[0], 4)
            dve.tensor_scalar(am[64:, :, 0, 0:C], am[64:, :, 0, 0:C], -1.0, None, ALU.mult)
            dve.tensor_scalar(am[0:64, :, 1, 0:C], am[0:64, :, 1, 0:C], -1.0, None, ALU.mult)
            dve.tensor_scalar(am[64:, :, 1, :], am[64:, :, 1, :], -1.0, None, ALU.mult).then_inc(f_neg, 1)
            for z in range(2):
                dve.wait_ge(s_ld[z], 16)
                v = stage[:, z].rearrange("p i r c -> p (i r c)")
                dve.tensor_reduce(ext[:, 2 * z:2 * z + 1], v, AX.X, ALU.max)
                dve.tensor_reduce(ext[:, 2 * z + 1:2 * z + 2], v, AX.X, ALU.min).then_inc(f_bm[z], 1)
            for u in range(16):
                dve.wait_ge(f_wp, u + 1)
                dve.tensor_copy(flat(wf[:, u // 8, 8 * (u % 8):8 * (u % 8) + 8, :]), ps[:, u % 8, :]).then_inc(f_we, 1)
            dve.wait_ge(f_we, 16)
            w_all = wf[:].rearrange("p z s y -> p (z s y)")
            dve.tensor_reduce(ext[:, 4:5], w_all, AX.X, ALU.max)
            dve.tensor_reduce(ext[:, 5:6], w_all, AX.X, ALU.min).then_inc(f_ext, 1)
            dve.wait_ge(f_top, 1)
            dve.tensor_reduce(mag[:, 0:1], top[:, 0:4], AX.X, ALU.max)
            dve.tensor_reduce(mag[:, 1:2], top[:, 4:6], AX.X, ALU.max).then_inc(k[1], 1)
            dve.wait_ge(k[1], 1)
            dve.tensor_scalar(mag[:], mag[:], 1e-30, None, ALU.max).then_inc(k[2], 1)
            dve.wait_ge(k[2], 1)
            dve.reciprocal(inv[:], mag[:]).then_inc(k[3], 1)
            dve.tensor_scalar(back[:], mag[:, 0:1], mag[:, 1:2], X_SCALE, ALU.mult, ALU.mult).then_inc(k[4], 1)
            dve.wait_ge(k[3], 1)
            dve.tensor_copy(sgn[:, 1:2], inv[:, 0:1])
            for t in range(0, 128, 32):
                d = dve.tensor_scalar(sgn[t:t + 32, 0:1], inv[t:t + 32, 0:1], 1.0 if t % 64 == 0 else -1.0, None,
                                      ALU.mult)
            d.then_inc(f_sc, 1)
            dve.wait_ge(k[4], 1)
            dve.tensor_scalar(am[:], am[:], back[:, 0:1], None, ALU.mult)
            dve.tensor_scalar(w_all, w_all, inv[:, 1:2], None, ALU.mult).then_inc(k[5], 1)
            dve.wait_ge(k[5], 1)
            dve.tensor_copy(w_st[:], wf[:]).then_inc(f_w, 1)
            dve.wait_ge(f_w, 1)
            for z in range(2):
                r = slice(64 - 64 * z, 128 - 64 * z)
                dve.tensor_tensor(w_st[r, z], wf[r, z], w_st[r, z], ALU.subtract)
            for n, (z, c) in enumerate(chunks):
                e = n % 2
                r = slice(64 * z, 64 * z + 64)
                dve.wait_ge(f_hi, 2 * n + 2)
                dve.tensor_tensor(b_lo[r, CH * c:CH * c + CH], stage[r, e], b_hi[r, z, CH * c:CH * c + CH],
                                  ALU.subtract).then_inc(f_lo[e], 1)


def modes(nc, spec, b_hi, b_lo, w_st, am, fd):
    with ExitStack() as ctx:
        def sb(name, shape, dt=F32):
            return ctx.enter_context(nc.sbuf_tensor(name, shape, dt))

        def sem(name):
            return ctx.enter_context(nc.semaphore(name))

        ring = ctx.enter_context(nc.psum_tensor("ring2", [128, 4, 2, 512], F32))
        wcur = sb("wcur", [128, 2, 2, MODES], F16)
        Mh = sb("Mh", [128, 2, MODES, 2 * RANK_I], F16)
        Ml = sb("Ml", [128, 2, MODES, 2 * RANK_I], F16)
        xin = sb("xin", [128, 2, B * 2 * MODES])
        xs = sb("xs", [128, 2, 2, B * 2, MODES], F16)
        pout = sb("pout", [128, 2, 2, B, MODES])
        ft = sb("ft", [128, 4, 2, 2, C])
        tmp = sb("tmp", [128, 2, 2, 2 * C])

        x_ld = [sem("xa_ld"), sem("xb_ld")]
        x_hi = [sem("xa_hi"), sem("xb_hi")]
        x_cv = [sem("xa_cv"), sem("xb_cv")]
        w_zero = sem("w_zero")
        w_cur = [sem("wa_cur"), sem("wb_cur")]
        p_bld = sem("p_bld")
        e_hi = sem("e_hi")
        e_lo = sem("e_lo")
        p_app = [sem("p_app0"), sem("p_app1")]
        e_app = [sem("e_app0"), sem("e_app1")]
        p_out = sem("p_out")
        e_out = sem("e_out")
        f_st = [sem("f_st0"), sem("f_st1")]
        k_tmp = sem("k_tmp")
        carried = sem("carried2")

        block = ctx.enter_context(nc.Block())

        @block.sync
        def _(sp):
            def load(s, z):
                sp.dma_start(xin[:, z], spec[bass.ds(64 * z + s, 1)].rearrange("s c b m -> (s c) (b m)")
                             ).then_inc(x_ld[z], 16)

            def store(s, u):
                sp.wait_ge(e_out, 2 * s + u + 1)
                for p in (2 * u, 2 * u + 1):
                    for z in range(2):
                        sp.dma_start(fd[128 * p:128 * p + 128, :, bass.ds(64 * z + s, 1), :]
                                     .rearrange("p r s o -> p r (s o)"), ft[:, p, z]).then_inc(f_st[u], 16)

            for z in range(2):
                load(0, z)
            for z in range(2):
                sp.wait_ge(x_cv[z], 1)
                load(1, z)
            with sp.Fori(1, MODES - 1) as s:
                store(s - 1, 0)
                store(s - 1, 1)
                for z in range(2):
                    sp.wait_ge(x_cv[z], s + 1)
                    load(s + 1, z)
            for s in (MODES - 2, MODES - 1):
                store(s, 0)
                store(s, 1)
            for u in range(2):
                sp.wait_ge(f_st[u], 64 * MODES)

        @block.gpsimd
        def _(pool):
            pool.memset(wcur[:], 0.0).then_inc(w_zero, 1)
            pool.wait_ge(w_zero, 1)

            def current(s, z):
                r = slice(64 * z, 64 * z + 64)
                pool.tensor_copy(wcur[:, z, 0, :], w_st[:, z, bass.ds(s, 1), :].rearrange("p s y -> p (s y)")
                                 ).then_inc(w_cur[z], 1)
                pool.wait_ge(w_cur[z], 2 * s + 1)
                carry(pool, carried)
                pool.tensor_copy(wcur[r, z, 1, :], w_st[r, z, bass.ds(s, 1), :].rearrange("p s y -> p (s y)")
                                 ).then_inc(w_cur[z], 1)
                pool.wait_ge(w_cur[z], 2 * s + 2)

            def convert(s, z):
                pool.wait_ge(x_ld[z], 16 * (s + 1))
                wait(pool, p_app[z], s)
                carry(pool, carried)
                hi = xs[:, z, 0].rearrange("p b y -> p (b y)")
                pool.tensor_copy(hi, xin[:, z]).then_inc(x_hi[z], 1)
                pool.wait_ge(x_hi[z], s + 1)
                pool.tensor_tensor(xs[:, z, 1].rearrange("p b y -> p (b y)"), xin[:, z], hi,
                                   ALU.subtract).then_inc(x_cv[z], 1)
                pool.wait_ge(x_cv[z], s + 1)

            current(0, 0)
            current(0, 1)
            convert(0, 0)
            convert(0, 1)
            with pool.Fori(1, MODES) as s:
                pool.wait_ge(p_bld, 16 * s - 8)
                current(s, 0)
                pool.wait_ge(p_bld, 16 * s)
                current(s, 1)
                convert(s, 0)
                convert(s, 1)
            carry(pool, carried)

        @block.tensor
        def _(pe):
            def build(s, n):
                z, u = divmod(n, 8)
                if u == 0:
                    pe.wait_ge(w_cur[z], 2 * s + 2)
                if n == 15:
                    pe.wait_ge(e_lo, 16 * s + 14)
                elif n >= 3:
                    pe.wait_ge(e_lo, 16 * s + n - 2)
                elif n == 0 and not isinstance(s, int):
                    pe.wait_ge(e_lo, 16 * s - 3)
                elif n == 1:
                    wait(pe, e_lo, 16 * s)
                for k in range(16):
                    m = 16 * u + k
                    o = ring[:, UNIT_PAIR[n], k // 8, 64 * (k % 8):64 * (k % 8) + 64]
                    pe.matmul(o, b_hi[:, z, m % 64, m // 64, :], wcur[:, z, 0, :], start=True, stop=False)
                    mm = pe.matmul(o, b_lo[:, m % 64, m // 64, :], wcur[:, z, 1, :], start=False, stop=True)
                mm.then_inc(p_bld, 1)

            def apply(s, z, part):
                if part == 0:
                    pe.wait_ge(e_lo, 16 * s + 8 * z + 8)
                    pe.wait_ge(x_cv[z], s + 1)
                    if z == 1:
                        pe.wait_ge(e_app[0], s + 1)
                    else:
                        wait(pe, e_out, 2 * s)
                for y in range(16 * part, 16 * part + 16):
                    o = ring[:, AUX, y // 32, 16 * (y % 32):16 * (y % 32) + 16]
                    pe.matmul(o, Mh[:, z, y, :], xs[:, z, 0, :, y], start=True, stop=False)
                    pe.matmul(o, Mh[:, z, y, :], xs[:, z, 1, :, y], start=False, stop=False)
                    mm = pe.matmul(o, Ml[:, z, y, :], xs[:, z, 0, :, y], start=False, stop=True)
                if part == 3:
                    mm.then_inc(p_app[z], 1)

            def out(s, u):
                if u == 0:
                    pe.wait_ge(e_app[1], s + 1)
                else:
                    pe.wait_ge(e_out, 2 * s + 1)
                for n in range(2):
                    p = 2 * u + n
                    for z in range(2):
                        for r in range(2):
                            mm = pe.matmul(ring[:, AUX, n, 256 * z:256 * z + 256],
                                           pout[:, z, r, 2 * p:2 * p + 2, :].rearrange("p b y -> p (b y)"),
                                           am[:, z, r, :], start=(r == 0), stop=(r == 1))
                mm.then_inc(p_out, 1)

            for n in range(16):
                build(0, n)
            for part in range(4):
                apply(0, 0, part)
            with pe.Fori(1, MODES) as s:
                for n in range(16):
                    build(s, n)
                    if 1 <= n <= 4:
                        apply(s - 1, 1, n - 1)
                    if n == OUT_AFTER[0]:
                        out(s - 1, 0)
                    if n == OUT_AFTER[1]:
                        out(s - 1, 1)
                    if 12 <= n <= 15:
                        apply(s, 0, n - 12)
            for part in range(4):
                apply(MODES - 1, 1, part)
            for u in range(2):
                out(MODES - 1, u)

        def unit(z, u):
            return (ring[:, UNIT_PAIR[8 * z + u]].rearrange("c k (m y) -> c (k m) y", y=MODES),
                    Mh[:, z, :, 16 * u:16 * u + 16].rearrange("c y m -> c m y"),
                    Ml[:, z, :, 16 * u:16 * u + 16].rearrange("c y m -> c m y"))

        @block.scalar
        def _(act):
            def build(s, n):
                act.wait_ge(p_bld, 16 * s + n + 1)
                ps, hi, _lo = unit(*divmod(n, 8))
                act.activation(hi, ps, ACT.Copy).then_inc(e_hi, 1)

            def apply(s, z):
                act.wait_ge(p_app[z], s + 1)
                act.activation(pout[:, z].rearrange("p r b y -> p y b r"),
                               ring[:, AUX].rearrange("p k (y b r) -> p (k y) b r", b=B, r=2),
                               ACT.Copy).then_inc(e_app[z], 1)

            for n in range(16):
                build(0, n)
            apply(0, 0)
            with act.Fori(1, MODES) as s:
                for n in range(16):
                    build(s, n)
                    if n == 4:
                        apply(s - 1, 1)
                    if n == 15:
                        apply(s, 0)
            apply(MODES - 1, 1)

        @block.vector
        def _(dve):
            def build(s, n):
                dve.wait_ge(e_hi, 16 * s + n + 1)
                ps, hi, lo = unit(*divmod(n, 8))
                dve.tensor_tensor(lo, ps, hi, ALU.subtract).then_inc(e_lo, 1)

            def out(s, u, alone=False):
                dve.wait_ge(p_out, 2 * s + u + 1)
                if not alone:
                    dve.wait_ge(f_st[u], 64 * s)
                ps = ring[:, AUX]
                o = ft[:, 2 * u:2 * u + 2].rearrange("p n z r o -> p n z (r o)")
                if alone:
                    dve.tensor_copy(o.rearrange("p n z m -> p n (z m)"), ps).then_inc(e_out, 1)
                else:
                    a, b, t = ps[:, :, 0:256], ps[:, :, 256:512], tmp[:, u]
                    dve.tensor_copy(t, b).then_inc(k_tmp, 1)
                    dve.wait_ge(k_tmp, 2 * (s - 1) + u + 1)
                    dve.tensor_tensor(o[:, :, 0, :], a, t, ALU.add)
                    dve.tensor_tensor(o[:, :, 1, 0:C], t[:, :, C:], a[:, :, C:], ALU.subtract)
                    dve.tensor_tensor(o[:, :, 1, C:], a[:, :, 0:C], t[:, :, 0:C], ALU.subtract).then_inc(e_out, 1)

            def iteration(s, alone=False):
                for n in range(16):
                    build(s, n)
                    for u in range(2):
                        if n == OUT_AFTER[u]:
                            out(s - 1, u, alone)

            for n in range(16):
                build(0, n)
            iteration(1, alone=True)
            with dve.Fori(2, MODES) as s:
                iteration(s)
            for u in range(2):
                out(MODES - 1, u)


def phase3(nc, fd, x1, iy_d, ix_d, out):
    with ExitStack() as ctx:
        def sb(name, shape):
            return ctx.enter_context(nc.sbuf_tensor(name, shape, F32))

        def sem(name):
            return ctx.enter_context(nc.semaphore(name))

        ring = ctx.enter_context(nc.psum_tensor("ring3", [128, 8, 512], F32))
        iy = sb("iy", [128, W])
        ix = sb("ix", [128, H])
        F = sb("F", [128, 2, 128, C])
        zb = sb("zb", [128, 2, IMGS * W])
        xq = sb("xq", [128, 4, HALF * IMGS, W])

        c_ld = sem("c_ld3")
        f_ld = [sem("f_ld0"), sem("f_ld1")]
        r_ld = sem("r_ld")
        p_z = sem("p_z")
        e_z = sem("e_z")
        p_o = sem("p_o")
        e_o = sem("e_o")
        o_st = [sem("o_st0"), sem("o_st1")]

        fd_v = fd.rearrange("(b y) r s o -> b (y r) (s o)", b=B)
        x1_v = x1.rearrange("n h w -> h n w")
        out_v = out.rearrange("b c h w -> h (b c) w")
        block = ctx.enter_context(nc.Block())

        @block.sync
        def _(sp):
            sp.dma_start(iy[:], iy_d).then_inc(c_ld, 16)
            sp.dma_start(ix[:], ix_d).then_inc(c_ld, 16)

            def load_f(b, e):
                sp.dma_start(F[:, e].rearrange("p s o -> p (s o)"),
                             fd_v[bass.ds(b, 1)].rearrange("b p m -> (b p) m"),
                             max_dma_last_dim=16384).then_inc(f_ld[e], 16)

            def load_x(h, e):
                for n in range(2):
                    sp.dma_start(xq[:, e, 8 * n:8 * n + 8, :],
                                 x1_v[:, bass.ds(16 * h + 8 * n, 8), :]).then_inc(r_ld, 16)

            def store(h, e):
                sp.wait_ge(e_o, 4 * (h + 1))
                sp.dma_start(out_v[:, bass.ds(16 * h, 16), :], xq[:, e]).then_inc(o_st[e % 2], 16)

            for e in range(2):
                sp.sem_inc(o_st[e], 16)
            load_f(0, 0)
            load_x(0, 0)
            sp.wait_ge(r_ld, 32)
            load_x(1, 1)
            load_f(1, 1)
            with sp.Fori(0, B // 2 - 1) as b2:
                for b in range(2):
                    for n in range(8):
                        h = 16 * b2 + 8 * b + n
                        sp.wait_ge(r_ld, 32 * (h + 2))
                        sp.wait_ge(o_st[n % 2], 16 * (8 * b2 + 4 * b + n // 2 + 1))
                        load_x(h + 2, (n + 2) % 4)
                        store(h, n % 4)
                    sp.wait_ge(p_z, 32 * (2 * b2 + b + 1))
                    load_f(2 * b2 + b + 2, b)
            for h in range(48, 64):
                if h < 62:
                    sp.wait_ge(r_ld, 32 * (h + 2))
                    sp.wait_ge(o_st[h % 2], 16 * (h // 2 + 1))
                    load_x(h + 2, (h + 2) % 4)
                store(h, h % 4)
            for e in range(2):
                sp.wait_ge(o_st[e], 16 * 33)

        @block.tensor
        def _(pe):
            pe.wait_ge(c_ld, 32)

            def quad(q, k, first):
                if k < 64:
                    if k % 32 == 0:
                        pe.wait_ge(f_ld[k // 32], first)
                    wait(pe, e_z, q - 3)
                    for m in range(IMGS):
                        mm = pe.matmul(ring[:, k % 4, 128 * m:128 * m + 128], F[:, k // 32, :, 4 * (k % 32) + m],
                                       iy[:], start=True, stop=True)
                    mm.then_inc(p_z, 1)

            def final(q, k):
                pe.wait_ge(e_z, q + 1)
                wait(pe, e_o, q - 3)
                pe.matmul(ring[:, 4 + k % 4, :], ix[:], zb[:, k % 2, :], start=True, stop=True).then_inc(p_o, 1)

            def pair(b2, start):
                for k in range(64):
                    quad(64 * b2 + k, k, 16 * (b2 + 1))
                    if not (start and k == 0):
                        final(64 * b2 + k - 1, (k - 1) % 4)

            pair(0, True)
            with pe.Fori(1, B // 2) as b2:
                pair(b2, False)
            final(NQ - 1, 3)

        @block.scalar
        def _(act):
            def quad(q, k):
                act.wait_ge(p_z, q + 1)
                wait(act, p_o, q - 1)
                act.activation(zb[:, k % 2, :], ring[:, k % 4, :], ACT.Copy).then_inc(e_z, 1)

            for k in range(4):
                quad(k, k)
            with act.Fori(1, NQ // 4) as i:
                for k in range(4):
                    quad(4 * i + k, k)

        @block.vector
        def _(dve):
            with dve.Fori(0, NQ // 16) as i:
                for k in range(16):
                    h = 4 * i + k // 4
                    dve.wait_ge(r_ld, 32 * (h + 1))
                    dve.wait_ge(p_o, 16 * i + k + 1)
                    x_ = xq[:, k // 4, 4 * (k % 4):4 * (k % 4) + 4, :].rearrange("p i w -> p (i w)")
                    dve.tensor_tensor(x_, x_, ring[:, 4 + k % 4, :], ALU.add).then_inc(e_o, 1)


def program(nc, x, ut, dt, dtail, mask, dfth, dftw, ones, bn, bst, cst, dst, am, iy, ix, out):
    x1 = nc.dram_tensor("x1", (B * C, H, W), F32, kind="Internal").ap()
    spec = nc.dram_tensor("spec", (128, C, B, 2 * MODES), F32, kind="Internal").ap()
    fd = nc.dram_tensor("fd", (B * MODES, 2, 128, C), F32, kind="Internal").ap()
    phase1(nc, x, ut, dt, dtail, mask, dfth, dftw, ones, x1, spec)
    phase2(nc, spec, bn, bst, cst, dst, am, fd)
    phase3(nc, fd, x1, iy, ix, out)


def layouts(inputs):
    import numpy as np

    f = np.asarray(inputs["L0_conv_f"])
    ut = np.zeros((H, UPS), np.float32)
    dT = np.zeros((UPS, H), np.float32)
    for i in range(H):
        ut[i, 2 * i:2 * i + TAPS] = f
        dT[2 * i:2 * i + TAPS, i] = f[::-1]
    dt = np.concatenate([dT[0:128, 0:LO], dT[128:256, HI0:]], axis=1)
    tail = dT[256:, TL0:]
    dtail = np.zeros((TR, IMGS * TLN + TLN), np.float32)
    mask = np.zeros((TR, TAIL, IMGS), np.float32)
    for m in range(IMGS):
        dtail[m::IMGS, TLN * m:TLN * m + TLN] = tail
        dtail[m::IMGS, IMGS * TLN:] = tail
        mask[m::IMGS, :, m] = 1.0
    n = np.arange(128)
    ang = 2 * np.pi * (np.outer(n, n) % 128) / 128
    cos, sin = np.cos(ang), np.sin(ang)
    dfth = np.concatenate([cos[:, 0:65], sin[:, 1:64]], axis=1)
    cy, sy = cos[:, 0:MODES], sin[:, 0:MODES]
    dftw = np.stack([np.concatenate([cy, -sy], 1), np.concatenate([-sy, -cy], 1)], axis=1)
    wt = np.full((MODES, 1), 2.0 / (H * W))
    wt[0] = 1.0 / (H * W)
    iy = np.stack([wt * cy.T, -wt * sy.T], axis=1).reshape(128, W)
    f32 = lambda a: np.ascontiguousarray(a, dtype=np.float32)

    bst, cst, dst, am = [], [], [], []
    rows = (np.arange(64), np.concatenate([[0], np.arange(63, 0, -1)]))
    for z in range(2):
        a, b, c, d = (np.asarray(inputs[f"L1_conv_{n}{z + 1}"]) for n in "abcd")
        b = b.transpose(3, 2, 0, 1)
        bst.append(np.concatenate([np.stack([b[0], b[1]], axis=2), np.stack([b[1], b[0]], axis=2)] * 2))
        c = c[:, rows[z]].transpose(3, 2, 1, 0)
        cst += [np.concatenate([c[0], c[1]] * 2, axis=2), np.concatenate([c[1], c[0]] * 2, axis=2)]
        dst += [d[:, :, 0, 0], d[:, :, 0, 1]]
        a = a[0].transpose(2, 1, 0)
        ri, ir = np.concatenate([a[0], a[1]], axis=1), np.concatenate([a[1], a[0]], axis=1)
        am.append(np.stack([np.concatenate([ri, ir]), np.concatenate([ir, ri])], axis=1))
    return {
        "x": np.ascontiguousarray(inputs["x"]), "ut": ut, "dt": f32(dt), "dtail": dtail, "mask": mask,
        "dfth": f32(dfth), "dftw": f32(dftw), "ones": np.full((128, 128), 1.0 / 128, np.float32),
        "bn": np.stack([np.asarray(inputs[f"L1_conv_b{z}"]).reshape(128, -1) for z in (1, 2)]),
        "bst": np.stack(bst), "cst": np.ascontiguousarray(np.concatenate(cst)),
        "dst": np.ascontiguousarray(np.concatenate(dst)), "am": np.ascontiguousarray(np.stack(am, axis=1)),
        "iy": f32(iy), "ix": f32(dfth.T),
    }


def kernel(**inputs):
    import concourse.bacc as _bacc
    from concourse import mybir as _mybir
    from concourse.bass_utils import run_bass_kernel_spmd as _run

    nc = _bacc.Bacc("TRN2", target_bir_lowering=False, num_devices=1, dynamic_dma_scratch_size=1024)
    arrays, args = {}, []
    for name, a in layouts(inputs).items():
        arrays[f"in_{name}"] = a
        args.append(nc.dram_tensor(f"in_{name}", a.shape, _mybir.dt.from_np(a.dtype), kind="ExternalInput").ap())
    args.append(nc.dram_tensor("out_0", (B, C, H, W), F32, kind="ExternalOutput").ap())
    program(nc, *args)
    return _run(nc, [arrays], core_ids=[0]).results[0]["out_0"]
```
